# Optimizing a Trainium2 kernel written in Bass

```python
import numpy as np
import jax
import jax.numpy as jnp

def _softmax(x, axis=-1):
    return jax.nn.softmax(x, axis=axis)

def _gelu(x):
    return jax.nn.gelu(x, approximate=True)

def _silu(x):
    return jax.nn.silu(x)

def _sigmoid(x):
    return jax.nn.sigmoid(x)

def _layernorm(x, axis=-1, eps=1e-05):
    m = jnp.mean(x, axis=axis, keepdims=True)
    v = jnp.var(x, axis=axis, keepdims=True)
    return (x - m) / jnp.sqrt(v + eps)

def _scatter_add(tgt, idx, src, axis=0):
    return tgt.at[idx].add(src)

def _segment_sum(src, seg, n):
    return jax.ops.segment_sum(src, seg, n)
kernel_name = 'mk_seq_postln_d1_jaxref_r8_e930ce'

def setup_inputs(seed: int=0):
    np.random.seed(seed)
    _w = jnp.asarray

    def _L0_attn_setup():
        import jax, jax.numpy as jnp
        import numpy as np
        from jax import lax
        B, T, H = (4, 128, 128)
        NH, KD, VD = (4, 64, 128)
        DK, DV = (KD // NH, VD // NH)
        R, R5, G = (32, 160, 64)
        EPS = 1e-05

        def _forward(h, x_proj_mu, xl_w1, xl_w2, xl_b2, x_out_w, x_bias, r_w, w_w1, w_w2, w_b, k_w, v_w, g_w, bonus, gn_weight, gn_bias, o_w):
            B_, T_, H_ = h.shape
            shifted = jnp.pad(h, ((0, 0), (1, 0), (0, 0)))[:, :T_]
            delta = shifted - h
            x_lerp = h + delta * x_proj_mu
            x0 = jnp.tanh(x_lerp @ xl_w1.T) @ xl_w2.T + xl_b2
            x1 = jnp.tanh(x0).reshape(B_, T_, 5, R)
            x2 = jnp.einsum('btnr,hnr->btnh', x1, x_out_w.reshape(H_, 5, R))
            mus = x2 + x_bias
            r_mu, w_mu, k_mu, v_mu, g_mu = (mus[:, :, i] for i in range(5))
            r = (h + delta * r_mu) @ r_w.T
            w_in = h + delta * w_mu
            w = jnp.tanh(w_in @ w_w1.T) @ w_w2.T + w_b
            k = (h + delta * k_mu) @ k_w.T
            v = (h + delta * v_mu) @ v_w.T
            g = (h + delta * g_mu) @ g_w.T
            r = r.reshape(B_, T_, NH, DK)
            k = k.reshape(B_, T_, NH, DK)
            v = v.reshape(B_, T_, NH, DV)
            wd = jnp.exp(-jnp.exp(w.reshape(B_, T_, NH, DK)))

            def step(S, xs):
                r_t, k_t, v_t, w_t = xs
                o_t = jnp.einsum('bhk,bhkv->bhv', r_t, S) + jnp.sum(r_t * bonus * k_t, -1, keepdims=True) * v_t
                S = S * w_t[..., None] + k_t[..., None] * v_t[..., None, :]
                return (S, o_t)
            xs = tuple((jnp.swapaxes(a, 0, 1) for a in (r, k, v, wd)))
            S0 = jnp.zeros((B_, NH, DK, DV), jnp.float32)
            _, oT = lax.scan(step, S0, xs)
            o = jnp.swapaxes(oT, 0, 1)
            mean = o.mean(-1, keepdims=True)
            var = o.var(-1, keepdims=True)
            o = ((o - mean) * lax.rsqrt(var + EPS)).reshape(B_, T_, VD)
            o = (o * gn_weight + gn_bias) * jax.nn.silu(g)
            return o @ o_w.T
        key = jax.random.key(seed)
        ks = jax.random.split(key, 20)
        n = lambda k, s, sc=0.02: jax.random.normal(k, s, dtype=jnp.float32) * sc
        return {'hidden_states': jax.random.normal(ks[0], (B, T, H), dtype=jnp.float32), 'x_proj_mu': n(ks[1], (H,), 0.1), 'xl_w1': n(ks[2], (R, H)), 'xl_w2': n(ks[3], (R5, R)), 'xl_b2': jnp.zeros((R5,), jnp.float32), 'x_out_w': n(ks[4], (H, R5)), 'x_bias': n(ks[5], (5, H), 0.1), 'r_w': n(ks[6], (KD, H)), 'w_w1': n(ks[7], (G, H)), 'w_w2': n(ks[8], (KD, G)), 'w_b': n(ks[9], (KD,), 0.1), 'k_w': n(ks[10], (KD, H)), 'v_w': n(ks[11], (VD, H)), 'g_w': n(ks[12], (VD, H)), 'bonus': n(ks[13], (NH, DK), 0.1), 'gn_weight': jnp.ones((VD,), jnp.float32), 'gn_bias': jnp.zeros((VD,), jnp.float32), 'o_w': n(ks[14], (H, VD))}
    _L0_attn_in = _L0_attn_setup()

    def _L0_ffn_setup():
        import jax, jax.numpy as jnp
        import numpy as np
        N_EMBD = 128
        N_EXPERTS = 16
        TOP_K = 2
        N_SHARED = 1
        HIDDEN = 4 * N_EMBD

        def _ffn(xf, w1, b1, w2, b2):
            h = jnp.maximum(xf @ w1 + b1, 0.0)
            return h @ w2 + b2
        key = jax.random.key(seed)
        ks = jax.random.split(key, 12)
        s = 0.02
        x = jax.random.normal(ks[0], (4, 256, N_EMBD), dtype=jnp.float32)
        router_w = jax.random.normal(ks[1], (N_EMBD, N_EXPERTS), dtype=jnp.float32) * s
        expert_bias = jnp.zeros((N_EXPERTS,), dtype=jnp.float32)
        shared_w1 = jax.random.normal(ks[2], (N_SHARED, N_EMBD, HIDDEN), dtype=jnp.float32) * s
        shared_b1 = jnp.zeros((N_SHARED, HIDDEN), dtype=jnp.float32)
        shared_w2 = jax.random.normal(ks[3], (N_SHARED, HIDDEN, N_EMBD), dtype=jnp.float32) * s
        shared_b2 = jnp.zeros((N_SHARED, N_EMBD), dtype=jnp.float32)
        routed_w1 = jax.random.normal(ks[4], (N_EXPERTS, N_EMBD, HIDDEN), dtype=jnp.float32) * s
        routed_b1 = jnp.zeros((N_EXPERTS, HIDDEN), dtype=jnp.float32)
        routed_w2 = jax.random.normal(ks[5], (N_EXPERTS, HIDDEN, N_EMBD), dtype=jnp.float32) * s
        routed_b2 = jnp.zeros((N_EXPERTS, N_EMBD), dtype=jnp.float32)
        return {'x': x, 'router_w': router_w, 'expert_bias': expert_bias, 'shared_w1': shared_w1, 'shared_b1': shared_b1, 'shared_w2': shared_w2, 'shared_b2': shared_b2, 'routed_w1': routed_w1, 'routed_b1': routed_b1, 'routed_w2': routed_w2, 'routed_b2': routed_b2}
    _L0_ffn_in = _L0_ffn_setup()
    _d = {'L0_attn_hidden_states': _L0_attn_in['hidden_states'], 'L0_attn_x_proj_mu': _L0_attn_in['x_proj_mu'], 'L0_attn_xl_w1': _L0_attn_in['xl_w1'], 'L0_attn_xl_w2': _L0_attn_in['xl_w2'], 'L0_attn_xl_b2': _L0_attn_in['xl_b2'], 'L0_attn_x_out_w': _L0_attn_in['x_out_w'], 'L0_attn_x_bias': _L0_attn_in['x_bias'], 'L0_attn_r_w': _L0_attn_in['r_w'], 'L0_attn_w_w1': _L0_attn_in['w_w1'], 'L0_attn_w_w2': _L0_attn_in['w_w2'], 'L0_attn_w_b': _L0_attn_in['w_b'], 'L0_attn_k_w': _L0_attn_in['k_w'], 'L0_attn_v_w': _L0_attn_in['v_w'], 'L0_attn_g_w': _L0_attn_in['g_w'], 'L0_attn_bonus': _L0_attn_in['bonus'], 'L0_attn_gn_weight': _L0_attn_in['gn_weight'], 'L0_attn_gn_bias': _L0_attn_in['gn_bias'], 'L0_attn_o_w': _L0_attn_in['o_w'], 'L0_ffn_router_w': _L0_ffn_in['router_w'], 'L0_ffn_expert_bias': _L0_ffn_in['expert_bias'], 'L0_ffn_shared_w1': _L0_ffn_in['shared_w1'], 'L0_ffn_shared_b1': _L0_ffn_in['shared_b1'], 'L0_ffn_shared_w2': _L0_ffn_in['shared_w2'], 'L0_ffn_shared_b2': _L0_ffn_in['shared_b2'], 'L0_ffn_routed_w1': _L0_ffn_in['routed_w1'], 'L0_ffn_routed_b1': _L0_ffn_in['routed_b1'], 'L0_ffn_routed_w2': _L0_ffn_in['routed_w2'], 'L0_ffn_routed_b2': _L0_ffn_in['routed_b2']}
    _x0 = _d['L0_attn_hidden_states']
    _d['L0_attn_hidden_states'] = jax.random.normal(jax.random.fold_in(jax.random.key(seed), 1), (32, 256, 128), dtype=_x0.dtype)
    del _x0
    return _d

def reference(L0_attn_hidden_states, L0_attn_x_proj_mu, L0_attn_xl_w1, L0_attn_xl_w2, L0_attn_xl_b2, L0_attn_x_out_w, L0_attn_x_bias, L0_attn_r_w, L0_attn_w_w1, L0_attn_w_w2, L0_attn_w_b, L0_attn_k_w, L0_attn_v_w, L0_attn_g_w, L0_attn_bonus, L0_attn_gn_weight, L0_attn_gn_bias, L0_attn_o_w, L0_ffn_router_w, L0_ffn_expert_bias, L0_ffn_shared_w1, L0_ffn_shared_b1, L0_ffn_shared_w2, L0_ffn_shared_b2, L0_ffn_routed_w1, L0_ffn_routed_b1, L0_ffn_routed_w2, L0_ffn_routed_b2):

    def _L0_attn_ref(hidden_states, x_proj_mu, xl_w1, xl_w2, xl_b2, x_out_w, x_bias, r_w, w_w1, w_w2, w_b, k_w, v_w, g_w, bonus, gn_weight, gn_bias, o_w):
        import jax, jax.numpy as jnp
        import numpy as np
        from jax import lax
        B, T, H = (4, 128, 128)
        NH, KD, VD = (4, 64, 128)
        DK, DV = (KD // NH, VD // NH)
        R, R5, G = (32, 160, 64)
        EPS = 1e-05

        def _forward(h, x_proj_mu, xl_w1, xl_w2, xl_b2, x_out_w, x_bias, r_w, w_w1, w_w2, w_b, k_w, v_w, g_w, bonus, gn_weight, gn_bias, o_w):
            B_, T_, H_ = h.shape
            shifted = jnp.pad(h, ((0, 0), (1, 0), (0, 0)))[:, :T_]
            delta = shifted - h
            x_lerp = h + delta * x_proj_mu
            x0 = jnp.tanh(x_lerp @ xl_w1.T) @ xl_w2.T + xl_b2
            x1 = jnp.tanh(x0).reshape(B_, T_, 5, R)
            x2 = jnp.einsum('btnr,hnr->btnh', x1, x_out_w.reshape(H_, 5, R))
            mus = x2 + x_bias
            r_mu, w_mu, k_mu, v_mu, g_mu = (mus[:, :, i] for i in range(5))
            r = (h + delta * r_mu) @ r_w.T
            w_in = h + delta * w_mu
            w = jnp.tanh(w_in @ w_w1.T) @ w_w2.T + w_b
            k = (h + delta * k_mu) @ k_w.T
            v = (h + delta * v_mu) @ v_w.T
            g = (h + delta * g_mu) @ g_w.T
            r = r.reshape(B_, T_, NH, DK)
            k = k.reshape(B_, T_, NH, DK)
            v = v.reshape(B_, T_, NH, DV)
            wd = jnp.exp(-jnp.exp(w.reshape(B_, T_, NH, DK)))

            def step(S, xs):
                r_t, k_t, v_t, w_t = xs
                o_t = jnp.einsum('bhk,bhkv->bhv', r_t, S) + jnp.sum(r_t * bonus * k_t, -1, keepdims=True) * v_t
                S = S * w_t[..., None] + k_t[..., None] * v_t[..., None, :]
                return (S, o_t)
            xs = tuple((jnp.swapaxes(a, 0, 1) for a in (r, k, v, wd)))
            S0 = jnp.zeros((B_, NH, DK, DV), jnp.float32)
            _, oT = lax.scan(step, S0, xs)
            o = jnp.swapaxes(oT, 0, 1)
            mean = o.mean(-1, keepdims=True)
            var = o.var(-1, keepdims=True)
            o = ((o - mean) * lax.rsqrt(var + EPS)).reshape(B_, T_, VD)
            o = (o * gn_weight + gn_bias) * jax.nn.silu(g)
            return o @ o_w.T
        return _forward(hidden_states, x_proj_mu, xl_w1, xl_w2, xl_b2, x_out_w, x_bias, r_w, w_w1, w_w2, w_b, k_w, v_w, g_w, bonus, gn_weight, gn_bias, o_w)

    def _L0_ffn_ref(x, router_w, expert_bias, shared_w1, shared_b1, shared_w2, shared_b2, routed_w1, routed_b1, routed_w2, routed_b2):
        import jax, jax.numpy as jnp
        import numpy as np
        N_EMBD = 128
        N_EXPERTS = 16
        TOP_K = 2
        N_SHARED = 1
        HIDDEN = 4 * N_EMBD

        def _ffn(xf, w1, b1, w2, b2):
            h = jnp.maximum(xf @ w1 + b1, 0.0)
            return h @ w2 + b2
        B, T, C = x.shape
        x_flat = x.reshape(-1, C)
        N = x_flat.shape[0]
        shared_out = jnp.zeros_like(x_flat)
        for s in range(N_SHARED):
            shared_out = shared_out + _ffn(x_flat, shared_w1[s], shared_b1[s], shared_w2[s], shared_b2[s])
        logits = x_flat @ router_w + expert_bias
        top_vals, top_idx = jax.lax.top_k(logits, TOP_K)
        weights = jax.nn.softmax(top_vals.astype(jnp.float32), axis=-1).astype(x.dtype)
        comb = jnp.zeros((N, N_EXPERTS), dtype=x.dtype)
        comb = comb.at[jnp.arange(N)[:, None], top_idx].add(weights)
        routed_out = jnp.zeros_like(x_flat)
        for e in range(N_EXPERTS):
            y_e = _ffn(x_flat, routed_w1[e], routed_b1[e], routed_w2[e], routed_b2[e])
            routed_out = routed_out + comb[:, e:e + 1] * y_e
        return (shared_out + routed_out).reshape(B, T, C)
    x = L0_attn_hidden_states
    x = _layernorm(x + _L0_attn_ref(x, L0_attn_x_proj_mu, L0_attn_xl_w1, L0_attn_xl_w2, L0_attn_xl_b2, L0_attn_x_out_w, L0_attn_x_bias, L0_attn_r_w, L0_attn_w_w1, L0_attn_w_w2, L0_attn_w_b, L0_attn_k_w, L0_attn_v_w, L0_attn_g_w, L0_attn_bonus, L0_attn_gn_weight, L0_attn_gn_bias, L0_attn_o_w), axis=-1)
    x = _layernorm(x + _L0_ffn_ref(x, L0_ffn_router_w, L0_ffn_expert_bias, L0_ffn_shared_w1, L0_ffn_shared_b1, L0_ffn_shared_w2, L0_ffn_shared_b2, L0_ffn_routed_w1, L0_ffn_routed_b1, L0_ffn_routed_w2, L0_ffn_routed_b2), axis=-1)
    return x

_drawn_inputs = setup_inputs


def setup_inputs(seed=0):
    import zlib

    import numpy as np

    out = dict(_drawn_inputs(seed))
    spreads = {'L0_attn_xl_b2': (0.0, 0.8),
     'L0_attn_gn_weight': (1.0, 0.6),
     'L0_attn_gn_bias': (0.0, 0.8),
     'L0_ffn_expert_bias': (0.0, 0.1),
     'L0_ffn_shared_b1': (0.0, 0.27),
     'L0_ffn_shared_b2': (0.0, 0.1),
     'L0_ffn_routed_b1': (0.0, 0.397),
     'L0_ffn_routed_b2': (0.0, 0.1)}
    factors = {'L0_attn_x_proj_mu': 8.0,
     'L0_attn_xl_w1': 8.0,
     'L0_attn_xl_w2': 8.0,
     'L0_attn_x_out_w': 8.0,
     'L0_attn_x_bias': 4.669,
     'L0_attn_w_w1': 22.397,
     'L0_attn_w_w2': 22.284,
     'L0_attn_w_b': 21.69,
     'L0_attn_bonus': 8.0}
    for name, (base, spread) in spreads.items():
        noise = np.random.default_rng([zlib.crc32(name.encode()), seed]).standard_normal(out[name].shape)
        drawn = base * np.exp(spread * noise) if base else spread * noise
        out[name] = jnp.asarray(drawn.astype(out[name].dtype))
    for name, factor in factors.items():
        out[name] = (out[name] * factor).astype(out[name].dtype)
    return out
```

```python
import numpy as np
import concourse.bass as bass
from concourse import mybir
from contextlib import ExitStack

SEQS, T, C = 32, 256, 128
NH, DK, DV = 4, 16, 32
HK, HV = NH * DK, NH * DV
RANK, NMIX = 32, 5
GATE = 64
N = SEQS * T
EXPERTS, TOPK, HIDDEN = 16, 2, 512
HC = HIDDEN // 128
EPS = 1e-5

UB = 2
UT = UB * T
UNITS = SEQS // UB
TILES = UT // 128
L = 32
NC = T // L
HALVES = [1, 2, 4, 8, 16]
ST = 256
SUB = ST // 128
RING = 4
ETILES = N * TOPK // ST + EXPERTS
CAP = N + ST
ROW = C + 4
AT_W, AT_DEST = C, C + 1
TRASH = N * TOPK

MIX_R, MIX_W, MIX_K, MIX_V, MIX_G = range(NMIX)
MIX_ORDER = [MIX_W, MIX_R, MIX_K, MIX_V, MIX_G]
MIX_BANK = {MIX_W: 0, MIX_R: 1, MIX_K: 1, MIX_V: 0, MIX_G: 0}

COLS = (["x_mu", "xl_b2a", "xl_b2b"] + [f"x_bias{n}" for n in range(NMIX)] + ["w_b", "bonus", "gn_w", "gn_b"]
        + [f"head{h}" for h in range(NH)] + [f"shared_b1_{c}" for c in range(HC)])
COL = {n: i for i, n in enumerate(COLS)}

MATS = {"xl_w1": (C, RANK), "xl_w2": (RANK, RANK * NMIX), "x_out_a": (128, C), "x_out_b": (RANK, C),
        "r_w": (C, HK), "k_w": (C, HK), "w_w1": (C, GATE), "w_w2": (GATE, HK), "v_w": (C, HV), "g_w": (C, HV),
        "o_w": (HV, C), "ident": (128, 128), "head_mean": (128, 128), "diag": (128, L),
        "before": (128, 128), "ones": (128, 128), "router_w": (C, EXPERTS), "expert_bias": (128, EXPERTS),
        "expert_no": (128, EXPERTS), "region": (128, EXPERTS), "token_no": (128, TILES * TOPK),
        "tile_no": (1, ETILES), "shared_b2": (128, C), "shared_w1": (C, HIDDEN), "shared_w2": (128, HIDDEN)}
MAT_AT, MAT_COLS = {}, 0
for _n, (_r, _c) in MATS.items():
    MAT_AT[_n] = MAT_COLS
    MAT_COLS += _c


def build(nc, hidden, mats_dram, cols_dram, masks_dram, w1_dram, w2_dram, b2_dram, out):
    f32, u32, i32 = mybir.dt.float32, mybir.dt.uint32, mybir.dt.int32
    ALU, ACT, AX = mybir.AluOpType, mybir.ActivationFunctionType, mybir.AxisListType
    hid_v = hidden.rearrange("b t c -> (b t) c").rearrange("(n p) c -> p n c", p=128)
    out_v = out.rearrange("b t c -> (b t) c").rearrange("(n p) c -> p n c", p=128)
    rows_dram = nc.dram_tensor("dispatched_rows", (EXPERTS * CAP + ST, ROW), f32).ap()
    back_dram = nc.dram_tensor("expert_results", (N * TOPK, C), f32).ap()
    back_v = back_dram.rearrange("(n p k) c -> p n (k c)", p=128, k=TOPK)
    ctx = ExitStack()
    with ctx:
        def sb(name, shape, dt=f32):
            return ctx.enter_context(nc.sbuf_tensor(name, shape, dt))

        def pb(name, shape, dt=f32):
            return ctx.enter_context(nc.psum_tensor(name, shape, dt))

        sems = {}

        def sem(name):
            if name not in sems:
                sems[name] = ctx.enter_context(nc.semaphore(name))
            return sems[name]

        mats = sb("mats", [128, MAT_COLS])
        cols = sb("cols", [128, len(COLS)])
        masks = sb("masks", [128, len(HALVES), L], u32)
        head_bonus = sb("head_bonus", [128, NH])

        def mat(name):
            r, c = MATS[name]
            return mats[0:r, MAT_AT[name]:MAT_AT[name] + c]

        def col(name, rows=128):
            return cols[0:rows, COL[name]:COL[name] + 1]

        def two(name, shape, dt=f32):
            return [sb(f"{name}_{i}", shape, dt) for i in range(2)]

        h_tok = sb("h_tok", [128, TILES, C])
        hT = sb("hT", [128, UB, T + 1])
        delta = sb("delta", [128, UB, T])
        x_lerp = sb("x_lerp", [128, UB, T])
        adapt0 = sb("adapt0", [RANK, UT])
        adapt1a = sb("adapt1a", [128, UT])
        adapt1b = sb("adapt1b", [RANK, UT])
        mixed_delta = sb("mixed_delta", [128, UB, T])
        mixed = two("mixed", [128, UB, T])
        decay_hid = sb("decay_hid", [GATE, UT])
        exp_w = sb("exp_w", [128, T])
        R1, K1, tot1 = two("R1", [128, T]), two("K1", [128, T]), two("tot1", [128, T])
        v_feat = sb("v_feat", [128, UT])
        v_tok = two("v_tok", [128, UB * NC, DV])
        v_block = sb("v_block", [128, UB * NC, NH, DV])
        gate_tanh = sb("gate_tanh", [128, UT])
        gate = two("gate", [128, UT])
        lv = ["1", "2", "4", "8", "16", "32"]
        Rl = {m: sb("R" + m, [128, T]) for m in lv[1:]}
        Kl = {m: sb("K" + m, [128, T]) for m in lv[1:]}
        tot = {m: sb("tot" + m, [128, T // int(m)]) for m in lv[1:]}
        r_fac = {m: sb("r_fac" + m, [128, T // (2 * int(m)), 2]) for m in lv[:-1]}
        k_fac = {m: sb("k_fac" + m, [128, T // (2 * int(m)), 2]) for m in lv[:-1]}
        k_heads = two("k_heads", [128, NC, NH, L])
        pair = sb("pair", [128, UB, NC * L])
        k_tok = sb("k_tok", [128, NC, 128])
        chunk_decay = sb("chunk_decay", [128, DV, NC])
        state = sb("state", [128, DV, NC])
        state_heads = sb("state_heads", [128, NC, NH, DV])
        o_sb = two("o_sb", [128, UT])
        h_res = sb("h_res", [128, TILES, C])
        norm_work = sb("norm_work", [128, 4, UT])
        o_cent, o_sq, o_std, o_norm = (norm_work[:, i, :] for i in range(4))
        o_aff = sb("o_aff", [128, UT])
        o_gated = sb("o_gated", [128, UT])
        z = sb("z", [128, TILES, C])
        stats = sb("stats", [128, TILES, 6])
        moments = sb("moments", [128, TILES, 2])
        z_std = sb("z_std", [128, TILES])
        minus_half = sb("minus_half", [128, TILES])
        z_rstd = sb("z_rstd", [128, TILES])
        eps = sb("eps", [128, 1])
        rows = [two(f"rows{k}", [128, TILES, ROW]) for k in range(TOPK)]
        x1T = sb("x1T", [128, UT])
        logits = sb("logits", [128, TILES, EXPERTS])
        top_val = sb("top_val", [128, TILES, 8])
        top_idx = sb("top_idx", [128, TILES, 8], u32)
        top_idf = sb("top_idf", [128, TILES, TOPK])
        top_gap = sb("top_gap", [128, TILES])
        top_exp = sb("top_exp", [128, TILES])
        top_sum = sb("top_sum", [128, TILES])
        top_w0 = sb("top_w0", [128, TILES])
        chosen = sb("chosen", [128, TILES, TOPK, EXPERTS])
        either = sb("either", [128, TILES, EXPERTS])
        seen = sb("seen", [128, TILES + 1, EXPERTS])
        place = sb("place", [128, TILES, EXPERTS])
        place_of = sb("place_of", [128, TILES, TOPK, EXPERTS])
        slot_f = sb("slot_f", [128, TILES, TOPK])
        slot = two("slot", [128, TILES, TOPK], u32)
        dest = sb("dest", [128, TILES, TOPK])
        hid = sb("hid", [128, HC, UT])
        x1_b2 = sb("x1_b2", [128, TILES, C])
        base_out = sb("base_out", [128, UNITS * TILES, C])
        w2_sb = sb("w2_sb", [128, EXPERTS, HC, C])
        b2_sb = norm_work[:, :, :].rearrange("p a b -> p (a b)").rearrange("p (e c) -> p e c", c=C)
        pad_rows = sb("pad_rows", [128, SUB, ROW])
        counts = sb("counts", [1, EXPERTS])
        ci = sb("ci", [1, 4, EXPERTS], i32)
        tiles_f = sb("tiles_f", [1, EXPERTS])
        tiles_to = sb("tiles_to", [1, EXPERTS])
        ones_row = sb("ones_row", [1, EXPERTS])
        pad_at_f = sb("pad_at_f", [1, EXPERTS])
        pad_at = sb("pad_at", [1, EXPERTS], i32)
        past = v_block[0:1, :, :, :].rearrange("p n h v -> p (n h v)")[:, 0:ETILES * EXPERTS].rearrange("p (n e) -> p n e", e=EXPERTS)
        past_n = past
        tile_e = sb("tile_e", [1, ETILES])
        tile_s = sb("tile_s", [1, ETILES])
        tile_v = sb("tile_v", [1, ETILES])
        tile_ei = sb("tile_ei", [1, ETILES], i32)
        tile_ri = sb("tile_ri", [1, ETILES], i32)
        hid_flat = hid[:, :, :].rearrange("p c t -> p (c t)")
        w1b = [hid_flat[:, i * (HIDDEN + HC):(i + 1) * (HIDDEN + HC)] for i in range(2)]
        row_in = [rows[i // 2][i % 2][:, 0:SUB, :] for i in range(RING)]
        xTe = [x1T[:, i * ST:(i + 1) * ST] for i in range(2)]
        hide = [k[:, :, :, :].rearrange("p c h s -> p (c h s)").rearrange("p (c t) -> p c t", t=ST) for k in k_heads]
        ye = [state_heads[:, i * SUB * C // HV:(i + 1) * SUB * C // HV, :, :].rearrange("p c h v -> p c (h v)") for i in range(2)]
        yw = [k_tok[:, SUB * i:SUB * (i + 1), :] for i in range(RING)]
        back = [v_block[:, :, :, :].rearrange("p n h v -> p (n h v)")[:, i * TILES * TOPK * C:(i + 1) * TILES * TOPK * C]
                .rearrange("p (n c) -> p n c", c=TOPK * C) for i in range(2)]
        as_rows = lambda t: t[:, :, :].rearrange("p b t -> p (b t)").rearrange("p (n c) -> p n c", c=C)
        f_sum, f_z = as_rows(delta), as_rows(x_lerp)
        f_out = [as_rows(m) for m in mixed]

        psP = [pb(f"psP{i}", [128, 512]) for i in range(2)]
        psL = [pb(f"psL{i}", [128, UB, 512]) for i in range(2)]
        psO = pb("psO", [128, UB, 512])
        O0, O1 = psO[:, 0, :], psO[:, 1, :]

        flat = lambda t: t.rearrange("p a b -> p (a b)")
        unflat = lambda t: t.rearrange("p (b t) -> p b t", b=UB)
        lay = lambda t: t.rearrange("p (c s) -> p c s", s=L)

        FIRST_LOOPED, END_LOOPED = 3, UNITS - 1

        class At:
            def __init__(self, off, regs=None):
                self.off, self.regs = off, regs
                self.par = (off + (FIRST_LOOPED if regs else 0)) % 2

            def to(self, d):
                return At(self.off + d, self.regs)

            def count(self, d):
                n = self.off + d
                return n if self.regs is None else self.regs[n]

            @property
            def index(self):
                return self.count(0)

        def done(eng, name, u):
            eng.wait_ge(sem(name), u.count(1))

        def before(eng, name, u, back=1):
            if u.regs is None and u.off + 1 - back < 1:
                return
            eng.wait_ge(sem(name), u.count(1 - back))

        def pipeline(eng, body):
            n = lambda u: At(u) if 0 <= u < UNITS else None
            for u in range(-1, FIRST_LOOPED):
                body(n(u + 1), n(u), n(u - 1))
            with eng.Fori(FIRST_LOOPED, END_LOOPED, 2) as u:
                regs = {0: u}
                for d in range(-3, 5):
                    if d:
                        regs[d] = eng.snap(u + d)
                for p in range(2):
                    a = At(p, regs)
                    body(a.to(1), a, a.to(-1))
            for u in range(END_LOOPED, UNITS + 1):
                body(n(u + 1), n(u), n(u - 1))

        block = ctx.enter_context(nc.Block())

        @block.sync
        def _(sp):
            sp.dma_start(mats[:, :], mats_dram).then_inc(sem("weights"), 16)
            sp.dma_start(cols[:, :], cols_dram).then_inc(sem("weights"), 16)
            sp.dma_start(masks[:, :, :], masks_dram).then_inc(sem("weights"), 16)
            sp.dma_start(w2_sb[:, :, :, :], w2_dram).then_inc(sem("expert_weights"), 16)
            def load_h(u):
                sp.wait_ge(sem("h_turned"), u + 1)
                sp.dma_start(h_tok[:, :, :], hid_v[:, bass.ds(u * TILES, TILES), :]).then_inc(sem("h_in"), 16)

            def load_res(u):
                sp.wait_ge(sem("h_res_used"), u + 1)
                sp.dma_start(h_res[:, :, :], hid_v[:, bass.ds(u * TILES, TILES), :]).then_inc(sem("h_res_in"), 16)
            load_h(0)
            load_h(1)
            with sp.Fori(0, UNITS - 2) as u:
                load_h(u + 2)
                load_res(u)
            load_res(UNITS - 2)
            load_res(UNITS - 1)
            sp.wait_ge(sem("base_out"), UNITS)
            sp.dma_start(b2_sb, b2_dram).then_inc(sem("expert_weights"), 16)
            for p in range(2):
                sp.wait_ge(sem(f"scattered{p}"), UNITS // 2 * TILES * TOPK * 16)
            sp.wait_ge(sem("pad_at"), 1)
            sp.wait_ge(sem("pad_rows"), 1)
            sp.dma_start(rows_dram[EXPERTS * CAP:EXPERTS * CAP + ST, :].rearrange("(s p) c -> p s c", p=128),
                         pad_rows[:, :, :]).then_inc(sem("padded"), 16)
            for e in range(EXPERTS):
                at = sp.value_load(pad_at[0:1, e:e + 1], min_val=e * CAP, max_val=e * CAP + N)
                sp.dma_start(rows_dram[bass.ds(at, ST), :].rearrange("(s p) c -> p s c", p=128),
                             pad_rows[:, :, :]).then_inc(sem("padded"), 16)
            sp.wait_ge(sem("padded"), (EXPERTS + 1) * 16)
            sp.wait_ge(sem("tile_table"), 1)

            def load_w1(j, i):
                p = i % 2
                if not (isinstance(j, int) and j < 2):
                    sp.wait_ge(sem("e_hid"), j - 1)
                sp.nop(nofuse=True)
                e = sp.value_load(tile_ei[0:1, bass.ds(j, 1)], min_val=0, max_val=EXPERTS - 1)
                sp.dma_start(w1b[p], w1_dram[bass.ds(e, 1), :, :].rearrange("e p n -> (e p) n")).then_inc(sem(f"e_w1_in{p}"), 16)

            def load_rows(j, i):
                if not (isinstance(j, int) and j < RING):
                    sp.wait_ge(sem(f"e_back{i}"), (j - i) * (SUB * 16 // RING))
                sp.nop(nofuse=True)
                r = sp.value_load(tile_ri[0:1, bass.ds(j, 1)], min_val=0, max_val=EXPERTS * CAP)
                sp.dma_start(row_in[i], rows_dram[bass.ds(r, ST), :].rearrange("(s p) c -> p s c", p=128)).then_inc(sem(f"e_rows_in{i}"), 16)
            for j in range(RING):
                load_rows(j, j)
                load_w1(j, j)
            with sp.Fori(1, ETILES // RING) as ring:
                for i in range(RING):
                    load_w1(sp.snap(ring * RING + i), i)
                    load_rows(sp.snap(ring * RING + i), i)
            for i in range(RING):
                sp.wait_ge(sem(f"e_back{i}"), ETILES // RING * SUB * 16)

            def load_back(u, p, guard):
                if guard is not None:
                    sp.wait_ge(sem("f_sum"), guard)
                    sp.nop(nofuse=True)
                sp.dma_start(back[p], back_v[:, bass.ds(u * TILES, TILES), :]).then_inc(sem(f"back_in{p}"), 16)
            for u in range(2):
                load_back(u, u, None)
            with sp.Fori(1, UNITS // 2) as half_u:
                u = sp.snap(half_u * 2)
                for p in range(2):
                    load_back(u + p, p, u + (p - 1))

        @block.tensor
        def _(pe):
            mm = nc.tensor.matmul
            pe.wait_ge(sem("weights"), 48)

            def by_seq(ps, w, x):
                pe.nop(nofuse=True)
                for b in range(UB):
                    i = mm(ps[64 * b:64 * b + 64, 0:T], w, x[:, b, :], start=True, stop=True)
                return i

            def mix(u, n):
                if n < 4:
                    w, a = mat("x_out_a")[32 * n:32 * n + 32, :], adapt1a[32 * n:32 * n + 32, :]
                else:
                    w, a = mat("x_out_b"), adapt1b[:, :]
                kw = {"tile_position": (96, 0)} if n == 3 else {}
                mm(psP[MIX_BANK[n]][:, :], w, a, start=True, stop=True, **kw).then_inc(sem(f"mix_ps{n}"))

            def a_turn(u):
                pe.wait_ge(sem("h_in"), u.count(1) * 16)
                before(pe, "gate", u)
                for j in range(TILES):
                    last = nc.tensor.transpose(psP[0][:, j * 128:(j + 1) * 128], h_tok[:, j, :], mat("ident"))
                last.then_inc(sem("h_turned"))

            def a_adapt0(u):
                before(pe, "v_feat", u)
                done(pe, "x_lerp", u)
                mm(psP[1][0:RANK, :], mat("xl_w1"), flat(x_lerp), start=True, stop=True).then_inc(sem("adapt0_ps"))

            def a_adapt1(u):
                done(pe, "adapt0", u)
                mm(psP[0][:, :], mat("xl_w2")[:, 0:128], adapt0[:, :], start=True, stop=True)
                mm(psP[1][0:RANK, :], mat("xl_w2")[:, 128:160], adapt0[:, :], start=True, stop=True).then_inc(sem("adapt1_ps"))

            def a_mix_w_r(u):
                done(pe, "adapt1", u)
                mix(u, MIX_W)
                mix(u, MIX_R)

            def a_decay_hid(u):
                done(pe, f"mixed{MIX_W}", u)
                mm(psP[0][0:GATE, :], mat("w_w1"), flat(mixed[0]), start=True, stop=True).then_inc(sem("decay_hid_ps"))

            def a_mix_k(u):
                done(pe, f"mixed{MIX_R}", u)
                mix(u, MIX_K)

            def a_r(u):
                done(pe, "decay_hid", u)
                by_seq(psP[0], mat("r_w"), mixed[1]).then_inc(sem("r_ps"))

            def a_w(u):
                done(pe, f"mixed{MIX_K}", u)
                by_seq(psP[1], mat("w_w2"), unflat(decay_hid[:, :])).then_inc(sem("w_ps"))

            def a_mix_v(u):
                done(pe, "r_done", u)
                mix(u, MIX_V)

            def a_k(u):
                done(pe, "exp_w", u)
                by_seq(psP[1], mat("k_w"), mixed[0]).then_inc(sem("k_ps"))

            def a_mix_g(u):
                done(pe, f"mixed{MIX_V}", u)
                mix(u, MIX_G)

            def a_v(u):
                done(pe, "k_done", u)
                mm(psP[1][:, :], mat("v_w"), flat(mixed[1]), start=True, stop=True).then_inc(sem("v_ps"))

            def a_g(u):
                done(pe, f"mixed{MIX_G}", u)
                mm(psP[0][:, :], mat("g_w"), flat(mixed[0]), start=True, stop=True).then_inc(sem("g_ps"))

            def b_level(u, j):
                m = lv[max(j - 1, 0)]
                R = R1[u.par] if m == "1" else Rl[m]
                done(pe, f"k_heads{j}", u)
                if j >= 2:
                    done(pe, f"r{m}", u)
                    done(pe, f"pair{j - 2}", u)
                else:
                    done(pe, "r_done", u)
                    before(pe, "state" if j else "k_tok", u)
                for b in range(UB):
                    for c in range(NC):
                        last = mm(psL[j % 2][:, b, c * L:(c + 1) * L],
                                  k_heads[j % 2][64 * b:64 * b + 64, c, :, :].rearrange("p h s -> p (h s)"),
                                  R[64 * b:64 * b + 64, c * L:(c + 1) * L], start=True, stop=True)
                last.then_inc(sem(f"level_ps{j}"))

            def b_k_tok(u):
                done(pe, "k_heads6", u)
                done(pe, "pair4", u)
                for c in range(NC):
                    last = nc.tensor.transpose(psL[0][:, c // 4, (c % 4) * 128:(c % 4 + 1) * 128],
                                               k_heads[0][:, c, :, :].rearrange("p h s -> p (h s)"), mat("ident"))
                last.then_inc(sem("k_tok_ps"))

            def b_kv(u):
                done(pe, "k_tok", u)
                done(pe, "v_tok", u)
                done(pe, "pair5", u)
                kv = psL[1][:, 0, 0:DV * NC].rearrange("p (v c) -> p v c", c=NC)
                for b in range(UB):
                    for c in range(NC):
                        last = mm(kv[64 * b:64 * b + 64, :, c], k_tok[:, c, 64 * b:64 * b + 64], v_tok[u.par][:, b * NC + c, :],
                                  start=True, stop=True)
                last.then_inc(sem("kv_ps"))

            def b_o(u, c_unit):
                done(pe, "state_heads", u)
                done(pe, "v_block", u)
                done(pe, "r32", u)
                if c_unit is not None:
                    done(pe, "base_out", c_unit)
                else:
                    before(pe, "o_sb", u)
                for b in range(UB):
                    for c in range(NC):
                        o = psO[:, b, c * L:(c + 1) * L]
                        last = mm(o, v_block[:, b * NC + c, :, :].rearrange("p h v -> p (h v)"), pair[:, b, c * L:(c + 1) * L],
                                  start=True, stop=(c == 0))
                        if c:
                            last = mm(o, state_heads[64 * b:64 * b + 64, c, :, :].rearrange("p h v -> p (h v)"),
                                      Rl["32"][64 * b:64 * b + 64, c * L:(c + 1) * L], start=False, stop=True)
                last.then_inc(sem("o_ps"))

            def c_mean(u):
                done(pe, "o_sb", u)
                mm(O0, mat("head_mean"), o_sb[u.par][:, :], start=True, stop=True).then_inc(sem("mean_ps"))

            def c_var(u):
                done(pe, "o_sq", u)
                mm(O1, mat("head_mean"), o_sq, start=True, stop=True).then_inc(sem("var_ps"))

            def c_attn(u):
                done(pe, "o_gated", u)
                for j in range(TILES):
                    last = mm(O0[:, j * 128:(j + 1) * 128], o_gated[:, j * 128:(j + 1) * 128], mat("o_w"), start=True, stop=True)
                last.then_inc(sem("attn_ps"))

            def c_turn(u):
                done(pe, "x1", u)
                for j in range(TILES):
                    last = nc.tensor.transpose(O1[:, j * 128:(j + 1) * 128], rows[0][u.par][:, j, 0:C], mat("ident"))
                last.then_inc(sem("x1T_ps"))

            def c_logits(u):
                done(pe, "x1T", u)
                for j in range(TILES):
                    last = mm(O0[:, j * EXPERTS:(j + 1) * EXPERTS], x1T[:, j * 128:(j + 1) * 128], mat("router_w"), start=True, stop=True)
                last.then_inc(sem("logits_ps"))

            def c_place(u):
                done(pe, "seen", u)
                ps = O0[:, 64:64 + TILES * EXPERTS]
                mm(ps, mat("before"), either[:, :, :].rearrange("p n e -> p (n e)"), start=True, stop=False)
                mm(ps, mat("ones"), seen[:, 0:TILES, :].rearrange("p n e -> p (n e)"), start=False, stop=True).then_inc(sem("place_ps"))

            def c_up(u, c):
                if c == 0:
                    done(pe, "x1T", u)
                elif c == 1:
                    done(pe, "place", u)
                else:
                    done(pe, f"hid{c - 2}", u)
                mm(O1 if c % 2 == 0 else O0, mat("shared_w1")[:, c * 128:(c + 1) * 128], x1T[:, :], start=True, stop=True).then_inc(sem(f"hid_ps{c}"))

            def c_down(u):
                for c in range(HC):
                    done(pe, f"hid{c}", u)
                for j in range(TILES):
                    for c in range(HC):
                        last = mm(O0[:, j * 128:(j + 1) * 128], hid[:, c, j * 128:(j + 1) * 128],
                                  mat("shared_w2")[:, c * 128:(c + 1) * 128], start=(c == 0), stop=(c == HC - 1))
                last.then_inc(sem("down_ps"))

            def body(a, b, c):
                if a: a_turn(a)
                if c: c_mean(c)
                if b: b_level(b, 0)
                if a: a_adapt0(a)
                if c: c_var(c)
                if b: b_level(b, 1)
                if a: a_adapt1(a)
                if b: b_level(b, 2)
                if a: a_mix_w_r(a)
                if c: c_attn(c)
                if b: b_level(b, 3)
                if a: a_decay_hid(a)
                if a: a_mix_k(a)
                if c: c_turn(c)
                if b: b_level(b, 4)
                if a: a_r(a)
                if c: c_logits(c)
                if a: a_w(a)
                if b: b_level(b, 5)
                if c: c_up(c, 0)
                if a: a_mix_v(a)
                if c: c_place(c)
                if b: b_k_tok(b)
                if c: c_up(c, 1)
                if a: a_k(a)
                if c: c_up(c, 2)
                if a: a_mix_g(a)
                if b: b_kv(b)
                if c: c_up(c, 3)
                if a: a_v(a)
                if a: a_g(a)
                if c: c_down(c)
                if b: b_o(b, c)

            pipeline(pe, body)
            pe.wait_ge(sem("base_out"), UNITS)
            pe.nop(nofuse=True)
            mm(O0[0:32, 0:EXPERTS], mat("ones")[:, 0:32], seen[:, TILES, :], start=True, stop=True).then_inc(sem("counts_ps"))

            pe.wait_ge(sem("expert_weights"), 32)
            pe.wait_ge(sem("tile_table"), 1)
            up_ps = lambda p: psL[p]

            def e_turn(j, i):
                pe.wait_ge(sem(f"e_rows_in{i}"), (j - i) * (16 // RING) + 16)
                for s in range(SUB):
                    last = nc.tensor.transpose(psP[i % 2][:, s * 128:(s + 1) * 128], row_in[i][:, s, 0:C], mat("ident"))
                last.then_inc(sem("e_turn_ps"))

            def e_up(j, i):
                p = i % 2
                pe.wait_ge(sem(f"e_w1_in{p}"), (j - p) * 8 + 16)
                pe.wait_ge(sem("e_xT"), j + 1)
                for c in range(HC):
                    last = mm(up_ps(p)[:, c // 2, (c % 2) * ST:(c % 2 + 1) * ST], w1b[p][:, c * 128:(c + 1) * 128], xTe[p],
                              start=True, stop=True)
                last.then_inc(sem("e_up_ps"))

            def e_down(j, i):
                p = i % 2
                pe.wait_ge(sem("e_hid"), j + 1)
                e = pe.value_load(tile_ei[0:1, bass.ds(j, 1)], min_val=0, max_val=EXPERTS - 1)
                for s in range(SUB):
                    for c in range(HC):
                        last = mm(psO[:, p, s * 128:(s + 1) * 128], hide[p][:, c, s * 128:(s + 1) * 128],
                                  w2_sb[:, bass.ds(e, 1), c, :].rearrange("p e c -> p (e c)"), start=(c == 0), stop=(c == HC - 1))
                last.then_inc(sem("e_down_ps"))

            e_turn(0, 0)
            e_turn(1, 1)
            e_up(0, 0)
            with pe.Fori(0, ETILES // RING - 1) as ring:
                for i in range(RING):
                    e_turn(pe.snap(ring * RING + (i + 2)), (i + 2) % RING)
                    e_up(pe.snap(ring * RING + (i + 1)), (i + 1) % RING)
                    e_down(pe.snap(ring * RING + i), i)
            for j in range(ETILES - RING, ETILES):
                if j + 2 < ETILES:
                    e_turn(j + 2, (j + 2) % RING)
                if j + 1 < ETILES:
                    e_up(j + 1, (j + 1) % RING)
                e_down(j, j % RING)

        @block.scalar
        def _(act):
            A = nc.scalar.activation
            act.wait_ge(sem("weights"), 48)
            act.wait_ge(sem("head_bonus"), 1)
            act.wait_ge(sem("zeroed"), 1)

            def a_adapt0(u):
                done(act, "adapt0_ps", u)
                A(adapt0[:, :], psP[1][0:RANK, :], ACT.Tanh).then_inc(sem("adapt0"))

            def a_adapt1(u):
                done(act, "adapt1_ps", u)
                A(adapt1a[:, :], psP[0][:, :], ACT.Tanh, bias=col("xl_b2a"))
                A(adapt1b[:, :], psP[1][0:RANK, :], ACT.Tanh, bias=col("xl_b2b", RANK)).then_inc(sem("adapt1"))

            def a_decay_hid(u):
                done(act, "decay_hid_ps", u)
                A(decay_hid[:, :], psP[0][0:GATE, :], ACT.Tanh).then_inc(sem("decay_hid"))

            def a_r(u):
                done(act, "r_ps", u)
                before(act, "level_ps1", u, 2)
                A(R1[u.par][:, :], psP[0][:, 0:T], ACT.Copy).then_inc(sem("r_done"))

            def a_w(u):
                done(act, "w_ps", u)
                before(act, "decay", u)
                A(exp_w[:, :], psP[1][:, 0:T], ACT.Exp, bias=col("w_b")).then_inc(sem("exp_w"))

            def a_decay(u):
                done(act, "exp_w", u)
                before(act, "tot2", u, 2)
                A(tot1[u.par][:, :], exp_w[:, :], ACT.Exp, scale=-1.0).then_inc(sem("decay"))

            def a_k(u):
                done(act, "k_ps", u)
                before(act, "r2", u, 2)
                A(K1[u.par][:, :], psP[1][:, 0:T], ACT.Copy).then_inc(sem("k_done"))

            def a_v(u):
                done(act, "v_ps", u)
                before(act, "v_tok", u)
                A(v_feat[:, :], psP[1][:, :], ACT.Copy).then_inc(sem("v_feat"))

            def a_g(u):
                done(act, "g_ps", u)
                A(gate_tanh[:, :], psP[0][:, :], ACT.Tanh, scale=0.5).then_inc(sem("gate_tanh"))

            def b_v_block(u):
                done(act, "v_tok", u)
                before(act, "o_ps", u)
                for h in range(NH):
                    p = slice(32 * h, 32 * h + 32)
                    last = A(v_block[p, :, h, :], v_tok[u.par][p, :, :], ACT.Copy)
                last.then_inc(sem("v_block"))

            def b_k_heads(u, j):
                m = lv[max(j - 1, 0)]
                K = K1[u.par] if m == "1" else Kl[m]
                if j >= 2:
                    done(act, f"level_ps{j - 2}", u)
                else:
                    before(act, "k_tok_ps" if j == 0 else "level_ps5", u)
                if j == 0:
                    done(act, "k_done", u)
                if j > 1:
                    done(act, f"r{m}", u)
                for h in range(NH):
                    last = A(k_heads[j % 2][:, :, h, :], lay(K[:, :]), ACT.Copy,
                             scale=head_bonus[:, h:h + 1] if j == 0 else col(f"head{h}"))
                last.then_inc(sem(f"k_heads{j}"))

            def b_k_tok(u):
                done(act, "k_tok_ps", u)
                A(k_tok[:, :, :], psL[0][:, :, :].rearrange("p b (c k) -> p (b c) k", k=128), ACT.Copy).then_inc(sem("k_tok"))

            def b_state_heads(u):
                done(act, "state", u)
                before(act, "o_ps", u)
                for h in range(NH):
                    last = A(state_heads[:, 1:NC, h, :], state[:, :, 0:NC - 1].rearrange("p v c -> p c v"), ACT.Copy, scale=col(f"head{h}"))
                last.then_inc(sem("state_heads"))

            def b_o(u):
                done(act, "o_ps", u)
                A(unflat(o_sb[u.par][:, :]), psO[:, :, 0:T], ACT.Copy).then_inc(sem("o_sb"))

            def c_sq(u):
                done(act, "o_cent", u)
                A(o_sq, o_cent, ACT.Square).then_inc(sem("o_sq"))

            def c_std(u):
                done(act, "var_ps", u)
                A(o_std, O1, ACT.Ln, bias=eps[:, 0:1]).then_inc(sem("o_log"))
                done(act, "o_log", u)
                A(o_std, o_std, ACT.Exp, scale=-0.5).then_inc(sem("o_std"))

            def c_aff(u):
                done(act, "o_norm", u)
                A(o_aff[:, :], o_norm, ACT.Identity, bias=col("gn_b"), scale=col("gn_w")).then_inc(sem("o_aff"))

            def c_x1T(u):
                done(act, "x1T_ps", u)
                A(x1T[:, :], O1, ACT.Copy).then_inc(sem("x1T"))

            def c_top_exp(u):
                done(act, "top_gap", u)
                A(top_exp[:, :], top_gap[:, :], ACT.Exp).then_inc(sem("top_exp"))

            def c_hid(u, c):
                done(act, f"hid_ps{c}", u)
                A(hid[:, c, :], O1 if c % 2 == 0 else O0, ACT.Relu, bias=col(f"shared_b1_{c}")).then_inc(sem(f"hid{c}"))

            def body(a, b, c):
                if b: b_v_block(b)
                if b: b_k_heads(b, 0)
                if c: c_sq(c)
                if b: b_k_heads(b, 1)
                if a: a_adapt0(a)
                if c: c_std(c)
                if b: b_k_heads(b, 2)
                if a: a_adapt1(a)
                if c: c_aff(c)
                if b: b_k_heads(b, 3)
                if a: a_decay_hid(a)
                if b: b_k_heads(b, 4)
                if a: a_r(a)
                if c: c_x1T(c)
                if a: a_w(a)
                if a: a_decay(a)
                if b: b_k_heads(b, 5)
                if c: c_top_exp(c)
                if c: c_hid(c, 0)
                if b: b_k_heads(b, 6)
                if c: c_hid(c, 1)
                if a: a_k(a)
                if b: b_k_tok(b)
                if c: c_hid(c, 2)
                if c: c_hid(c, 3)
                if a: a_v(a)
                if a: a_g(a)
                if b: b_state_heads(b)
                if b: b_o(b)

            pipeline(act, body)

            def e_hid(j, i):
                p = i % 2
                act.wait_ge(sem("e_up_ps"), j + 1)
                for c in range(HC):
                    last = A(hide[p][:, c, :], psL[p][:, c // 2, (c % 2) * ST:(c % 2 + 1) * ST], ACT.Relu,
                             bias=w1b[p][:, HIDDEN + c:HIDDEN + c + 1])
                last.then_inc(sem("e_hid"))

            def e_weigh(j, i):
                p = i % 2
                act.wait_ge(sem("e_y"), j + 1)
                for s in range(SUB):
                    last = A(yw[i][:, s, :], ye[p][:, s, :], ACT.Copy, scale=row_in[i][:, s, AT_W:AT_W + 1])
                last.then_inc(sem("e_yw"))

            e_hid(0, 0)
            with act.Fori(0, ETILES // RING - 1) as ring:
                for i in range(RING):
                    e_hid(act.snap(ring * RING + (i + 1)), (i + 1) % RING)
                    e_weigh(act.snap(ring * RING + i), i)
            for j in range(ETILES - RING, ETILES):
                if j + 1 < ETILES:
                    e_hid(j + 1, (j + 1) % RING)
                e_weigh(j, j % RING)

            with act.Fori(0, UNITS // 2) as half_u:
                u = act.snap(half_u * 2)
                for p in range(2):
                    act.wait_ge(sem("f_out"), u + (p + 1))
                    act.dma_start(out_v[:, bass.ds(u * TILES + p * TILES, TILES), :], f_out[p]).then_inc(sem(f"stored{p}"), 16)
            for p in range(2):
                act.wait_ge(sem(f"stored{p}"), UNITS // 2 * 16 + 16)

        @block.gpsimd
        def _(pool):
            G = nc.gpsimd
            pool.sem_inc(sem("h_turned"), 1)
            pool.sem_inc(sem("stored0"), 16)
            pool.sem_inc(sem("stored1"), 16)
            pool.sem_inc(sem("h_res_used"), 1)
            for m in lv[:-1]:
                G.memset(r_fac[m][:, :, 0], 1.0)
                G.memset(k_fac[m][:, :, 1], 1.0)
            G.memset(chunk_decay[:, :, 0], 0.0)
            G.memset(eps[:, :], EPS)
            G.memset(minus_half[:, :], -0.5)
            G.memset(hT[:, :, 0:1], 0.0)
            G.memset(seen[:, 0, :], 0.0)
            G.memset(ones_row[:, :], 1.0)
            for k in range(TOPK):
                for p in range(2):
                    G.memset(rows[k][p][:, :, :], 0.0)
            G.memset(pad_rows[:, :, :], 0.0)
            G.memset(v_block[:, :, :, :], 0.0).then_inc(sem("zeroed"))
            pool.wait_ge(sem("weights"), 48)
            pool.wait_ge(sem("zeroed"), 1)
            G.tensor_copy(dest[:, :, :].rearrange("p n k -> p (n k)"), mat("token_no")).then_inc(sem("dest0"))
            G.iota(pad_rows[:, :, AT_DEST:AT_DEST + 1].bitcast(i32), pattern=[[0, SUB], [1, 1]], base=TRASH, channel_multiplier=1).then_inc(sem("pad_rows"))

            def b_factor(u, i):
                m, m2 = lv[i], lv[i + 1]
                w = int(m)
                t_m, K, R = (tot1[u.par], K1[u.par], R1[u.par]) if w == 1 else (tot[m], Kl[m], Rl[m])
                pairs = t_m[:, :].rearrange("p (n two) -> p n two", two=2)
                blocks = lambda t: t[:, :].rearrange("p (n two w) -> p n two w", two=2, w=w)
                fac = lambda t: t[:, :, :].unsqueeze(3).broadcast_to([128, T // (2 * w), 2, w])
                if w > 1:
                    done(pool, f"tot{m}", u)
                else:
                    done(pool, "decay", u)
                    before(pool, "chunk_decay", u)
                pool.nop(nofuse=True)
                G.tensor_copy(r_fac[m][:, :, 1], pairs[:, :, 0])
                G.tensor_copy(k_fac[m][:, :, 0], pairs[:, :, 1])
                G.tensor_tensor(tot[m2][:, :], pairs[:, :, 0], pairs[:, :, 1], ALU.mult).then_inc(sem(f"tot{m2}"))
                if w == 1:
                    done(pool, "k_done", u)
                    done(pool, "r_done", u)
                else:
                    done(pool, f"r{m}", u)
                done(pool, f"tot{m2}", u)
                before(pool, f"k_heads{i + 2}", u)
                G.tensor_tensor(blocks(Kl[m2]), blocks(K), fac(k_fac[m]), ALU.mult)
                before(pool, f"level_ps{i + 2}" if m2 != "32" else "o_ps", u)
                G.tensor_tensor(blocks(Rl[m2]), blocks(R), fac(r_fac[m]), ALU.mult).then_inc(sem(f"r{m2}"))

            def b_chunk_decay(u):
                done(pool, "tot32", u)
                before(pool, "state", u)
                pool.nop(nofuse=True)
                G.tensor_copy(chunk_decay[:, :, 1:NC],
                              tot["32"][:, 1:NC].unsqueeze(1).broadcast_to([128, DV, NC - 1])).then_inc(sem("chunk_decay"))

            def c_rstd(u):
                done(pool, "moments", u)
                pool.nop(nofuse=True)
                G.tensor_scalar(z_std[:, :], moments[:, :, 1], EPS, None, ALU.add).then_inc(sem("var_eps"))
                done(pool, "var_eps", u)
                G.tensor_tensor(z_rstd[:, :], z_std[:, :], minus_half[:, :], ALU.pow).then_inc(sem("z_rstd"))

            def c_rows(u):
                done(pool, "x1", u)
                before(pool, "base_out", u)
                pool.nop(nofuse=True)
                G.tensor_copy(rows[1][u.par][:, :, 0:C], rows[0][u.par][:, :, 0:C]).then_inc(sem("rows1"))
                G.tensor_tensor(x1_b2[:, :, :], rows[0][u.par][:, :, 0:C], mat("shared_b2").unsqueeze(1).broadcast_to([128, TILES, C]),
                                ALU.add).then_inc(sem("x1_b2"))

            def c_scatter(u):
                done(pool, "slots", u)
                done(pool, "rows1", u)
                pool.nop(nofuse=True)
                for j in range(TILES):
                    for k in range(TOPK):
                        G.indirect_dma_start(rows_dram[:, :], bass.IndirectOffsetOnAxis(slot[u.par][:, j, k:k + 1], 0),
                                             rows[k][u.par][:, j, :], None).then_inc(sem(f"scattered{u.par}"), 16)

            def body(a, b, c):
                if b: b_factor(b, 0)
                if b: b_factor(b, 1)
                if b: b_factor(b, 2)
                if c: c_rstd(c)
                if b: b_factor(b, 3)
                if c: c_rows(c)
                if b: b_factor(b, 4)
                if b: b_chunk_decay(b)
                if c: c_scatter(c)

            pipeline(pool, body)

            with pool.Fori(0, ETILES // RING) as ring:
                for i in range(RING):
                    pool.wait_ge(sem("e_yw"), ring * RING + (i + 1))
                    pool.nop(nofuse=True)
                    for s in range(SUB):
                        G.indirect_dma_start(back_dram[:, :], bass.IndirectOffsetOnAxis(row_in[i][:, s, AT_DEST:AT_DEST + 1].bitcast(u32), 0),
                                             yw[i][:, s, :], None, bounds_check=TRASH - 1, oob_is_err=False).then_inc(sem(f"e_back{i}"), 16)

            with pool.Fori(0, UNITS // 2) as half_u:
                u = pool.snap(half_u * 2)
                for p in range(2):
                    pool.wait_ge(sem("f_moments"), u + (p + 1))
                    pool.nop(nofuse=True)
                    G.tensor_scalar(z_std[:, :], moments[:, :, 1], EPS, None, ALU.add).then_inc(sem("f_var_eps"))
                    pool.wait_ge(sem("f_var_eps"), u + (p + 1))
                    G.tensor_tensor(z_rstd[:, :], z_std[:, :], minus_half[:, :], ALU.pow).then_inc(sem("f_rstd"))

        @block.vector
        def _(dve):
            V = nc.vector
            dve.wait_ge(sem("weights"), 48)
            V.tensor_scalar(head_bonus[:, :], cols[:, COL["head0"]:COL["head0"] + NH], col("bonus"), None, ALU.mult).then_inc(sem("head_bonus"))
            dve.wait_ge(sem("zeroed"), 1)
            dve.wait_ge(sem("dest0"), 1)

            def a_delta(u):
                dve.wait_ge(sem("h_turned"), u.count(2))
                before(dve, f"mixed{MIX_G}", u)
                V.tensor_copy(hT[:, :, 1:T + 1], unflat(psP[0][:, :])).then_inc(sem("hT"))
                done(dve, "hT", u)
                V.tensor_tensor(delta[:, :, :], hT[:, :, 0:T], hT[:, :, 1:T + 1], ALU.subtract).then_inc(sem("delta"))
                done(dve, "delta", u)
                before(dve, "adapt0_ps", u)
                V.scalar_tensor_tensor(x_lerp[:, :, :], delta[:, :, :], col("x_mu"), hT[:, :, 1:T + 1], ALU.mult, ALU.add).then_inc(sem("x_lerp"))

            def a_mixed(u, i):
                n = MIX_ORDER[i]
                (done if i else before)(dve, f"mixed{MIX_ORDER[i - 1]}", u)
                done(dve, f"mix_ps{n}", u)
                V.scalar_tensor_tensor(mixed_delta[:, :, :], unflat(psP[MIX_BANK[n]][:, :]),
                                       col(f"x_bias{n}"), delta[:, :, :], ALU.add, ALU.mult).then_inc(sem(f"mixed_delta{n}"))
                done(dve, f"mixed_delta{n}", u)
                if i >= 2:
                    done(dve, ["decay_hid_ps", "r_ps", "k_ps"][i - 2], u)
                else:
                    before(dve, ["g_ps", "v_ps"][i], u)
                V.tensor_tensor(mixed[i % 2][:, :, :], mixed_delta[:, :, :], hT[:, :, 1:T + 1], ALU.add).then_inc(sem(f"mixed{n}"))

            def a_v_tok(u):
                done(dve, "v_feat", u)
                before(dve, "kv_ps", u, 2)
                V.transpose(v_tok[u.par][:, :, :].rearrange("p n v -> p (n v)"), v_feat[:, :]).then_inc(sem("v_tok"))

            def a_gate(u):
                done(dve, "gate_tanh", u)
                before(dve, "o_gated", u, 2)
                V.scalar_tensor_tensor(gate[u.par][:, :], gate_tanh[:, :], 1.0, psP[0][:, :], ALU.add, ALU.mult).then_inc(sem("gate"))

            def b_pair(u, j):
                done(dve, f"level_ps{j}", u)
                ps = psL[j % 2][:, :, 0:T].rearrange("p b (c t) -> p b c t", t=L)
                to = pair[:, :, :].rearrange("p b (c t) -> p b c t", t=L)
                if j == 0:
                    before(dve, "o_ps", u)
                    m = mat("diag").unsqueeze(1).unsqueeze(1).broadcast_to([128, UB, NC, L])
                    V.tensor_tensor(to, ps, m, ALU.mult).then_inc(sem("pair0"))
                else:
                    m = masks[:, j - 1, :].unsqueeze(1).unsqueeze(1).broadcast_to([128, UB, NC, L])
                    done(dve, f"pair{j - 1}", u)
                    dve.nop(nofuse=True)
                    V.copy_predicated(to, m, ps).then_inc(sem(f"pair{j}"))

            def b_state(u):
                done(dve, "kv_ps", u)
                done(dve, "chunk_decay", u)
                before(dve, "state_heads", u)
                V.tensor_tensor_scan(state[:, :, :].rearrange("p v c -> p (v c)"), chunk_decay[:, :, :].rearrange("p v c -> p (v c)"),
                                     psL[1][:, 0, 0:DV * NC], 0.0, ALU.mult, ALU.add).then_inc(sem("state"))

            def c_cent(u):
                done(dve, "mean_ps", u)
                before(dve, "o_norm", u)
                V.tensor_tensor(o_cent, o_sb[u.par][:, :], O0, ALU.subtract).then_inc(sem("o_cent"))

            def c_norm(u):
                done(dve, "o_std", u)
                before(dve, "o_aff", u)
                V.tensor_tensor(o_norm, o_cent, o_std, ALU.mult).then_inc(sem("o_norm"))

            def c_gated(u):
                done(dve, "o_aff", u)
                before(dve, "attn_ps", u)
                V.scalar_tensor_tensor(o_gated[:, :], o_aff[:, :], 0.5, gate[u.par][:, :], ALU.mult, ALU.mult).then_inc(sem("o_gated"))

            def layer_norm(zt, to, name):
                pass

            def c_z(u):
                done(dve, "attn_ps", u)
                dve.wait_ge(sem("h_res_in"), u.count(1) * 16)
                before(dve, "x1", u)
                V.tensor_tensor(flat(z[:, :, :]), O0, flat(h_res[:, :, :]), ALU.add).then_inc(sem("h_res_used"))
                dve.wait_ge(sem("h_res_used"), u.count(2))
                for j in range(TILES):
                    last = V.bn_stats(stats[:, j, :], z[:, j, :])
                last.then_inc(sem("stats"))
                done(dve, "stats", u)
                dve.nop(nofuse=True)
                for j in range(TILES):
                    last = V.bn_aggr(moments[:, j, :], stats[:, j, :])
                last.then_inc(sem("moments"))

            def scattered(u, back):
                if u.regs is None and u.off + 1 - back < 1:
                    return
                dve.wait_ge(sem(f"scattered{u.par}"), u.count(-u.par) * (TILES * TOPK * 8))

            def c_x1(u):
                done(dve, "z_rstd", u)
                scattered(u, 2)
                before(dve, "rows1", u, 2)
                for j in range(TILES):
                    last = V.tensor_scalar(rows[0][u.par][:, j, 0:C], z[:, j, :], moments[:, j, 0:1], z_rstd[:, j:j + 1],
                                           ALU.subtract, ALU.mult)
                last.then_inc(sem("x1"))

            ROUTE = ["logits", "top_val", "top_idf", "chosen", "either", "seen0", "seen1", "seen2",
                     "place_of", "slot_f", "top_sum", "top_w0", "dest_out"]

            def routed(u, name):
                dve.wait_ge(sem("route_steps"), u.index * len(ROUTE) + (ROUTE.index(name) + 1))

            def c_top(u):
                done(dve, "logits_ps", u)
                before(dve, "slots", u)
                V.tensor_tensor(logits[:, :, :], O0[:, 0:TILES * EXPERTS].rearrange("p (n e) -> p n e", e=EXPERTS),
                                mat("expert_bias").unsqueeze(1).broadcast_to([128, TILES, EXPERTS]), ALU.add).then_inc(sem("route_steps"))
                routed(u, "logits")
                dve.nop(nofuse=True)
                for j in range(TILES):
                    last = V.max(top_val[:, j, :], logits[:, j, :])
                last.then_inc(sem("route_steps"))
                routed(u, "top_val")
                dve.nop(nofuse=True)
                for j in range(TILES):
                    last = V.max_index(top_idx[:, j, :], top_val[:, j, :], logits[:, j, :])
                V.tensor_tensor(top_gap[:, :], top_val[:, :, 1], top_val[:, :, 0], ALU.subtract).then_inc(sem("top_gap"))
                done(dve, "top_gap", u)
                V.tensor_copy(top_idf[:, :, :], top_idx[:, :, 0:TOPK]).then_inc(sem("route_steps"))
                routed(u, "top_idf")
                V.tensor_tensor(chosen[:, :, :, :], top_idf[:, :, :].unsqueeze(3).broadcast_to([128, TILES, TOPK, EXPERTS]),
                                mat("expert_no").unsqueeze(1).unsqueeze(1).broadcast_to([128, TILES, TOPK, EXPERTS]),
                                ALU.is_equal).then_inc(sem("route_steps"))
                routed(u, "chosen")
                V.tensor_tensor(either[:, :, :], chosen[:, :, 0, :], chosen[:, :, 1, :], ALU.add).then_inc(sem("route_steps"))
                routed(u, "either")
                for j in range(TILES):
                    V.tensor_tensor(seen[:, j + 1, :], seen[:, j, :], either[:, j, :], ALU.add).then_inc(sem("route_steps" if j < TILES - 1 else "seen"))
                    if j < TILES - 1:
                        routed(u, f"seen{j}")

            def c_slots(u):
                done(dve, "place_ps", u)
                V.tensor_tensor(place[:, :, :], O0[:, 64:64 + TILES * EXPERTS].rearrange("p (n e) -> p n e", e=EXPERTS),
                                mat("region").unsqueeze(1).broadcast_to([128, TILES, EXPERTS]), ALU.add).then_inc(sem("place"))
                V.tensor_copy(seen[:, 0, :], seen[:, TILES, :])
                done(dve, "place", u)
                V.tensor_tensor(place_of[:, :, :, :], chosen[:, :, :, :], place[:, :, :].unsqueeze(2).broadcast_to([128, TILES, TOPK, EXPERTS]),
                                ALU.mult).then_inc(sem("route_steps"))
                routed(u, "place_of")
                V.tensor_reduce(slot_f[:, :, :], place_of[:, :, :, :], AX.X, ALU.add).then_inc(sem("route_steps"))
                routed(u, "slot_f")
                scattered(u, 2)
                V.tensor_copy(slot[u.par][:, :, :], slot_f[:, :, :])
                done(dve, "top_exp", u)
                V.tensor_scalar(top_sum[:, :], top_exp[:, :], 1.0, None, ALU.add).then_inc(sem("route_steps"))
                routed(u, "top_sum")
                V.reciprocal(top_w0[:, :], top_sum[:, :]).then_inc(sem("route_steps"))
                routed(u, "top_w0")
                V.tensor_copy(rows[0][u.par][:, :, AT_W], top_w0[:, :])
                V.tensor_tensor(rows[1][u.par][:, :, AT_W], top_w0[:, :], top_exp[:, :], ALU.mult)
                for k in range(TOPK):
                    last = V.tensor_copy(rows[k][u.par][:, :, AT_DEST].bitcast(i32), dest[:, :, k])
                last.then_inc(sem("route_steps"))
                routed(u, "dest_out")
                V.tensor_scalar(dest[:, :, :], dest[:, :, :], float(TOPK * UT), None, ALU.add).then_inc(sem("slots"))

            def c_base(u):
                done(dve, "down_ps", u)
                done(dve, "x1_b2", u)
                i = u.index
                V.tensor_tensor(base_out[:, bass.ds(i * TILES, TILES), :].rearrange("p n c -> p (n c)"), O0, flat(x1_b2[:, :, :]), ALU.add).then_inc(sem("base_out"))

            def body(a, b, c):
                if c: c_cent(c)
                if a: a_delta(a)
                if b: b_pair(b, 0)
                if c: c_norm(c)
                if b: b_pair(b, 1)
                if c: c_gated(c)
                if b: b_pair(b, 2)
                if a: a_mixed(a, 0)
                if a: a_mixed(a, 1)
                if c: c_z(c)
                if b: b_pair(b, 3)
                if c: c_x1(c)
                if a: a_mixed(a, 2)
                if b: b_pair(b, 4)
                if c: c_top(c)
                if b: b_pair(b, 5)
                if a: a_mixed(a, 3)
                if c: c_slots(c)
                if a: a_mixed(a, 4)
                if b: b_state(b)
                if a: a_v_tok(a)
                if a: a_gate(a)
                if c: c_base(c)

            pipeline(dve, body)

            step = [0]

            def link(ins):
                step[0] += 1
                ins.then_inc(sem("table_step"))
                dve.wait_ge(sem("table_step"), step[0])

            dve.wait_ge(sem("counts_ps"), 1)
            link(V.tensor_copy(counts[:, :], O0[0:1, 0:EXPERTS]))
            link(V.tensor_scalar(tiles_f[:, :], counts[:, :], float(ST - 1), None, ALU.add))
            link(V.tensor_copy(ci[:, 0, :], tiles_f[:, :]))
            link(V.tensor_scalar(ci[:, 1, :], ci[:, 0, :], ST.bit_length() - 1, None, ALU.logical_shift_right))
            link(V.tensor_copy(tiles_f[:, :], ci[:, 1, :]))
            link(V.tensor_tensor_scan(tiles_to[:, :], ones_row[:, :], tiles_f[:, :], 0.0, ALU.mult, ALU.add))
            link(V.tensor_tensor(pad_at_f[:, :], counts[:, :], mat("region")[0:1, :], ALU.add))
            V.tensor_copy(pad_at[:, :], pad_at_f[:, :]).then_inc(sem("pad_at"))
            t_bc = mat("tile_no").unsqueeze(2).broadcast_to([1, ETILES, EXPERTS])
            link(V.tensor_tensor(past, t_bc, tiles_to[:, :].unsqueeze(1).broadcast_to([1, ETILES, EXPERTS]), ALU.is_ge))
            link(V.tensor_reduce(tile_e[:, :], past, AX.X, ALU.add))
            link(V.tensor_tensor(past_n, past, tiles_f[:, :].unsqueeze(1).broadcast_to([1, ETILES, EXPERTS]), ALU.mult))
            link(V.tensor_reduce(tile_s[:, :], past_n, AX.X, ALU.add))
            link(V.tensor_tensor(tile_s[:, :], mat("tile_no"), tile_s[:, :], ALU.subtract))
            link(V.tensor_scalar(tile_v[:, :], tile_e[:, :], float(EXPERTS), float(ST), ALU.is_lt, ALU.mult))
            link(V.tensor_tensor(tile_s[:, :], tile_s[:, :], tile_v[:, :], ALU.mult))
            link(V.tensor_scalar(tile_v[:, :], tile_e[:, :], float(CAP), None, ALU.mult))
            link(V.tensor_tensor(tile_s[:, :], tile_s[:, :], tile_v[:, :], ALU.add))
            link(V.tensor_scalar(tile_e[:, :], tile_e[:, :], float(EXPERTS - 1), None, ALU.min))
            link(V.tensor_copy(tile_ri[:, :], tile_s[:, :]))
            V.tensor_copy(tile_ei[:, :], tile_e[:, :]).then_inc(sem("tile_table"))
            dve.wait_ge(sem("tile_table"), 1)
            dve.wait_ge(sem("expert_weights"), 32)

            def e_xT(j, p):
                dve.wait_ge(sem("e_turn_ps"), j + 1)
                V.tensor_copy(xTe[p], psP[p][:, 0:ST]).then_inc(sem("e_xT"))

            def e_y(j, p):
                dve.wait_ge(sem("e_down_ps"), j + 1)
                e = dve.value_load(tile_ei[0:1, bass.ds(j, 1)], min_val=0, max_val=EXPERTS - 1)
                V.tensor_tensor(ye[p], psO[:, p, 0:ST].rearrange("p (s c) -> p s c", c=C),
                                b2_sb[:, bass.ds(e, 1), :].broadcast_to([128, SUB, C]), ALU.add).then_inc(sem("e_y"))

            e_xT(0, 0)
            e_xT(1, 1)
            with dve.Fori(0, ETILES // 2 - 1) as half_j:
                for p in range(2):
                    dve.wait_ge(sem("e_up_ps"), half_j * 2 + (p + 1))
                    e_xT(dve.snap(half_j * 2 + (p + 2)), p)
                    e_y(dve.snap(half_j * 2 + p), p)
            for j in range(ETILES - 2, ETILES):
                e_y(j, j % 2)

            with dve.Fori(0, UNITS // 2) as half_u:
                u = dve.snap(half_u * 2)
                n16 = dve.snap((u + 2) * 8)
                for p in range(2):
                    dve.wait_ge(sem(f"back_in{p}"), n16)
                    V.tensor_tensor(f_sum, back[p][:, :, 0:C], back[p][:, :, C:2 * C], ALU.add).then_inc(sem("f_sum"))
                    dve.wait_ge(sem("f_sum"), u + (p + 1))
                    V.tensor_tensor(flat(f_z), flat(f_sum),
                                    base_out[:, bass.ds(u * TILES + p * TILES, TILES), :].rearrange("p n c -> p (n c)"), ALU.add).then_inc(sem("f_z"))
                    dve.wait_ge(sem("f_z"), u + (p + 1))
                    for j in range(TILES):
                        last = V.bn_stats(stats[:, j, :], f_z[:, j, :])
                    last.then_inc(sem("f_stats"))
                    dve.wait_ge(sem("f_stats"), u + (p + 1))
                    dve.nop(nofuse=True)
                    for j in range(TILES):
                        last = V.bn_aggr(moments[:, j, :], stats[:, j, :])
                    last.then_inc(sem("f_moments"))
                    dve.wait_ge(sem("f_rstd"), u + (p + 1))
                    dve.wait_ge(sem(f"stored{p}"), n16)
                    for j in range(TILES):
                        last = V.tensor_scalar(f_out[p][:, j, :], f_z[:, j, :], moments[:, j, 0:1], z_rstd[:, j:j + 1],
                                               ALU.subtract, ALU.mult)
                    last.then_inc(sem("f_out"))


def pack(i):
    m = np.zeros((128, MAT_COLS), np.float32)

    def put(name, a):
        r, c = MATS[name]
        m[:r, MAT_AT[name]:MAT_AT[name] + c] = a
    g = lambda n: np.asarray(i["L0_attn_" + n])
    f = lambda n: np.asarray(i["L0_ffn_" + n])
    put("xl_w1", g("xl_w1").T)
    put("xl_w2", g("xl_w2").T)
    put("x_out_a", g("x_out_w").T[:128])
    put("x_out_b", g("x_out_w").T[128:])
    for n in ("r_w", "k_w", "w_w1", "w_w2", "v_w", "g_w", "o_w"):
        put(n, g(n).T)
    p = np.arange(128)
    put("ident", np.eye(128, dtype=np.float32))
    put("head_mean", (p[:, None] // DV == p[None, :] // DV).astype(np.float32) / DV)
    put("diag", (p[:, None] % L == np.arange(L)[None, :]).astype(np.float32))
    put("before", (p[:, None] < p[None, :]).astype(np.float32))
    put("ones", np.ones((128, 128), np.float32))
    put("router_w", f("router_w"))
    put("expert_bias", np.broadcast_to(f("expert_bias"), (128, EXPERTS)))
    put("expert_no", np.broadcast_to(np.arange(EXPERTS, dtype=np.float32), (128, EXPERTS)))
    put("region", np.broadcast_to(np.arange(EXPERTS, dtype=np.float32) * CAP, (128, EXPERTS)))
    n = (np.arange(TILES)[None, :, None] * 128 + p[:, None, None]) * TOPK + np.arange(TOPK)
    put("token_no", n.reshape(128, -1).astype(np.float32))
    put("tile_no", np.arange(ETILES, dtype=np.float32)[None])
    put("shared_b2", np.broadcast_to(f("shared_b2")[0], (128, C)))
    put("shared_w1", f("shared_w1")[0])
    put("shared_w2", f("shared_w2")[0].reshape(HC, 128, C).transpose(1, 0, 2).reshape(128, HIDDEN))
    c = np.zeros((128, len(COLS)), np.float32)

    def putc(name, a):
        c[:len(a), COL[name]] = a
    putc("x_mu", g("x_proj_mu"))
    putc("xl_b2a", g("xl_b2")[:128])
    putc("xl_b2b", g("xl_b2")[128:])
    for n in range(NMIX):
        putc(f"x_bias{n}", g("x_bias")[n])
    putc("w_b", np.tile(g("w_b"), UB))
    putc("bonus", np.tile(g("bonus").reshape(-1), UB))
    putc("gn_w", g("gn_weight"))
    putc("gn_b", g("gn_bias"))
    for h in range(NH):
        putc(f"head{h}", ((p % HK) // DK == h).astype(np.float32))
    for h in range(HC):
        putc(f"shared_b1_{h}", f("shared_b1")[0][h * 128:(h + 1) * 128])
    s, t = p[:, None] % L, np.arange(L)[None, :]
    masks = np.stack([((s // w) % 2 == 0) & (t // w == s // w + 1) for w in HALVES], 1).astype(np.uint32)
    b1 = f("routed_b1").reshape(EXPERTS, HC, 128).transpose(0, 2, 1)
    w1 = np.ascontiguousarray(np.concatenate([f("routed_w1"), b1], axis=2))
    w2 = np.ascontiguousarray(f("routed_w2").reshape(EXPERTS, HC, 128, C).transpose(2, 0, 1, 3))
    b2 = np.ascontiguousarray(np.broadcast_to(f("routed_b2"), (128, EXPERTS, C)))
    return {"in_mats": m, "in_cols": c, "in_masks": masks, "in_w1": w1, "in_w2": w2, "in_b2": b2}


def kernel(**inputs):
    import concourse.bacc as _bacc
    from concourse.bass_utils import run_bass_kernel_spmd as _run
    nc = _bacc.Bacc("TRN2", target_bir_lowering=False, num_devices=1)
    arrays = {"in_hidden": np.ascontiguousarray(inputs["L0_attn_hidden_states"]), **pack(inputs)}
    aps = [nc.dram_tensor(n, a.shape, mybir.dt.from_np(a.dtype), kind="ExternalInput").ap() for n, a in arrays.items()]
    out = nc.dram_tensor("out", (SEQS, T, C), mybir.dt.float32, kind="ExternalOutput").ap()
    build(nc, *aps, out)
    r = _run(nc, [arrays], core_ids=[0])
    return r.results[0]["out"]
```

```python
import numpy as np
import concourse.bass as bass
from concourse import mybir
from contextlib import ExitStack

SEQS, T, C = 32, 256, 128
NH, DK, DV = 4, 16, 32
HK, HV = NH * DK, NH * DV
RANK, NMIX = 32, 5
GATE = 64
N = SEQS * T
EXPERTS, TOPK, HIDDEN = 16, 2, 512
HC = HIDDEN // 128
EPS = 1e-5

UB = 2
UT = UB * T
UNITS = SEQS // UB
TILES = UT // 128
L = 32
NC = T // L
HALVES = [1, 2, 4, 8, 16]
ST = 256
SUB = ST // 128
RING = 8
W_RING = 4
ETILES = N * TOPK // ST + EXPERTS
CAP = N + ST
ROW = C + 4
AT_W, AT_DEST = C, C + 1
TRASH = N * TOPK

MIX_R, MIX_W, MIX_K, MIX_V, MIX_G = range(NMIX)
MIX_ORDER = [MIX_W, MIX_R, MIX_K, MIX_V, MIX_G]
MIX_BANK = {MIX_W: 0, MIX_R: 1, MIX_K: 1, MIX_V: 0, MIX_G: 0}

COLS = (["x_mu", "xl_b2a", "xl_b2b"] + [f"x_bias{n}" for n in range(NMIX)] + ["w_b", "bonus", "gn_w", "gn_b"]
        + [f"head{h}" for h in range(NH)] + [f"shared_b1_{c}" for c in range(HC)])
COL = {n: i for i, n in enumerate(COLS)}

MATS = {"xl_w1": (C, RANK), "xl_w2": (RANK, RANK * NMIX), "x_out_a": (128, C), "x_out_b": (RANK, C),
        "r_w": (C, HK), "k_w": (C, HK), "w_w1": (C, GATE), "w_w2": (UB * GATE, HK), "v_w": (C, HV), "g_w": (C, HV),
        "o_w": (HV, C), "ident": (128, 128), "head_mean": (128, 128), "diag": (128, L),
        "before": (128, 128), "ones": (128, 128), "router_w": (C, EXPERTS), "expert_bias": (128, EXPERTS),
        "expert_no": (128, EXPERTS), "region": (128, EXPERTS), "token_no": (128, TILES * TOPK),
        "tile_no": (1, ETILES), "shared_b2": (128, C), "shared_w1": (C, HIDDEN), "shared_w2": (128, HIDDEN)}
MAT_AT, MAT_COLS = {}, 0
for _n, (_r, _c) in MATS.items():
    MAT_AT[_n] = MAT_COLS
    MAT_COLS += _c


def build(nc, hidden, mats_dram, cols_dram, masks_dram, w1_dram, w2_dram, b2_dram, out):
    f32, u32, i32 = mybir.dt.float32, mybir.dt.uint32, mybir.dt.int32
    ALU, ACT, AX = mybir.AluOpType, mybir.ActivationFunctionType, mybir.AxisListType
    hid_v = hidden.rearrange("b t c -> (b t) c").rearrange("(n p) c -> p n c", p=128)
    out_v = out.rearrange("b t c -> (b t) c").rearrange("(n p) c -> p n c", p=128)
    rows_dram = nc.dram_tensor("dispatched_rows", (EXPERTS * CAP + ST, ROW), f32).ap()
    back_dram = nc.dram_tensor("expert_results", (N * TOPK, C), f32).ap()
    back_v = back_dram.rearrange("(n p k) c -> p n (k c)", p=128, k=TOPK)
    ctx = ExitStack()
    with ctx:
        def sb(name, shape, dt=f32):
            return ctx.enter_context(nc.sbuf_tensor(name, shape, dt))

        def pb(name, shape, dt=f32):
            return ctx.enter_context(nc.psum_tensor(name, shape, dt))

        sems = {}

        def sem(name):
            if name not in sems:
                sems[name] = ctx.enter_context(nc.semaphore(name))
            return sems[name]

        mats = sb("mats", [128, MAT_COLS])
        cols = sb("cols", [128, len(COLS)])
        masks = sb("masks", [128, len(HALVES), L], u32)
        head_bonus = sb("head_bonus", [128, NH])

        def mat(name):
            r, c = MATS[name]
            return mats[0:r, MAT_AT[name]:MAT_AT[name] + c]

        def col(name, rows=128):
            return cols[0:rows, COL[name]:COL[name] + 1]

        def two(name, shape, dt=f32):
            return [sb(f"{name}_{i}", shape, dt) for i in range(2)]

        h_tok = sb("h_tok", [128, TILES, C])
        hT = sb("hT", [128, UB, T + 1])
        delta = sb("delta", [128, UB, T])
        x_lerp = sb("x_lerp", [128, UB, T])
        adapt0 = sb("adapt0", [RANK, UT])
        adapt1a = sb("adapt1a", [128, UT])
        adapt1b = sb("adapt1b", [RANK, UT])
        mixed = two("mixed", [128, UB, T])
        decay_hid = sb("decay_hid", [UB * GATE, T])
        exp_w = sb("exp_w", [128, T])
        R1 = two("R1", [128, UB, T])
        K1, tot1 = two("K1", [128, T]), two("tot1", [128, T])
        v_feat = sb("v_feat", [128, UT])
        v_tok = two("v_tok", [128, UB * NC, DV])
        v_block = sb("v_block", [128, UB * NC, NH, DV])
        gate = two("gate", [128, UT])
        lv = ["1", "2", "4", "8", "16", "32"]
        Rl = {m: sb("R" + m, [128, UB, T]) for m in lv[1:]}
        Kl = {m: sb("K" + m, [128, T]) for m in lv[1:]}
        tot = {m: sb("tot" + m, [128, T // int(m)]) for m in lv[1:]}
        r_fac = {m: sb("r_fac" + m, [128, T // (2 * int(m)), 2]) for m in lv[:-1]}
        k_fac = {m: sb("k_fac" + m, [128, T // (2 * int(m)), 2]) for m in lv[:-1]}
        k_heads = two("k_heads", [128, NC, NH, L])
        pair = sb("pair", [128, UB, NC * L])
        k_tok = sb("k_tok", [128, NC, 128])
        chunk_decay = sb("chunk_decay", [128, DV, NC])
        state = sb("state", [128, DV, NC])
        state_heads = sb("state_heads", [128, NC, NH, DV])
        o_sb = two("o_sb", [128, UT])
        h_res = sb("h_res", [128, TILES, C])
        norm_work = sb("norm_work", [128, 4, UT])
        o_cent, o_std, o_aff, o_gated = (norm_work[:, i, :] for i in range(4))
        o_norm, o_sq = o_cent, o_std
        z = sb("z", [128, TILES, C])
        stats = sb("stats", [128, TILES, 6])
        moments = sb("moments", [128, TILES, 2])
        z_var = sb("z_var", [128, TILES])
        minus_half = sb("minus_half", [128, TILES])
        z_rstd = sb("z_rstd", [128, TILES])
        eps = sb("eps", [128, 1])
        rows = [two(f"rows{k}", [128, TILES, ROW]) for k in range(TOPK)]
        x1T = sb("x1T", [128, UT])
        logits = sb("logits", [128, TILES, EXPERTS])
        top_val = sb("top_val", [128, TILES, 8])
        top_idx = sb("top_idx", [128, TILES, 8], u32)
        top_idf = sb("top_idf", [128, TILES, TOPK])
        top_gap = sb("top_gap", [128, TILES])
        top_exp = sb("top_exp", [128, TILES])
        top_sum = sb("top_sum", [128, TILES])
        top_w0 = sb("top_w0", [128, TILES])
        chosen = sb("chosen", [128, TILES, TOPK, EXPERTS])
        either = sb("either", [128, TILES, EXPERTS])
        seen = sb("seen", [128, TILES + 1, EXPERTS])
        place = sb("place", [128, TILES, EXPERTS])
        place_of = sb("place_of", [128, TILES, TOPK, EXPERTS])
        slot_f = sb("slot_f", [128, TILES, TOPK])
        slot = two("slot", [128, TILES, TOPK], u32)
        dest = sb("dest", [128, TILES, TOPK])
        hid = sb("hid", [128, HC, UT])
        base_out = sb("base_out", [128, UNITS * TILES, C])
        w2_sb = sb("w2_sb", [128, EXPERTS, HC, C])
        b2_sb = norm_work[:, :, :].rearrange("p a b -> p (a b)").rearrange("p (e c) -> p e c", c=C)
        pad_rows = sb("pad_rows", [128, SUB, ROW])
        counts = sb("counts", [1, EXPERTS])
        ci = sb("ci", [1, 4, EXPERTS], i32)
        tiles_f = sb("tiles_f", [1, EXPERTS])
        tiles_to = sb("tiles_to", [1, EXPERTS])
        ones_row = sb("ones_row", [1, EXPERTS])
        pad_at_f = sb("pad_at_f", [1, EXPERTS])
        pad_at = sb("pad_at", [1, EXPERTS], i32)
        past = v_block[0:1, :, :, :].rearrange("p n h v -> p (n h v)")[:, 0:ETILES * EXPERTS].rearrange("p (n e) -> p n e", e=EXPERTS)
        tile_e = sb("tile_e", [1, ETILES])
        tile_s = sb("tile_s", [1, ETILES])
        tile_v = sb("tile_v", [1, ETILES])
        tile_ei = sb("tile_ei", [1, ETILES], i32)
        tile_ri = sb("tile_ri", [1, ETILES], i32)
        hid_flat = hid[:, :, :].rearrange("p c t -> p (c t)")
        v_block_flat = v_block[:, :, :, :].rearrange("p n h v -> p (n h v)")
        w1b = [(hid_flat, v_block_flat)[i // 2][:, (i % 2) * (HIDDEN + HC):(i % 2 + 1) * (HIDDEN + HC)] for i in range(W_RING)]
        row_in = [rows[i // 4][i // 2 % 2][:, i % 2 * SUB:(i % 2 + 1) * SUB, :] for i in range(RING)]
        xTe = [x1T[:, i * ST:(i + 1) * ST] for i in range(2)]
        hide = [k[:, :, :, :].rearrange("p c h s -> p (c h s)").rearrange("p (c t) -> p c t", t=ST) for k in k_heads]
        ye = [state_heads[:, i * SUB * C // HV:(i + 1) * SUB * C // HV, :, :].rearrange("p c h v -> p c (h v)") for i in range(2)]
        yw_pairs = [R[:, :, :].rearrange("p b (s c) -> p b s c", c=C) for R in (R1[0], R1[1], Rl["2"], Rl["4"])]
        yw = [yw_pairs[i // 2][:, i % 2, :, :] for i in range(RING)]
        BACK_RING = 4
        back = [t.rearrange("p (n c) -> p n c", c=TOPK * C) for t in (
            v_block_flat[:, 0:TILES * TOPK * C], v_block_flat[:, TILES * TOPK * C:2 * TILES * TOPK * C],
            *(k[:, :, :, :].rearrange("p c h s -> p (c h s)") for k in k_heads))]
        f_sum, f_z = ([hid[:, 2 * p + i, :] for p in range(2)] for i in range(2))
        f_out = [m[:, :, :].rearrange("p b t -> p (b t)").rearrange("p (n c) -> p n c", c=C) for m in mixed]
        f_stats, f_moments = two("f_stats", [128, TILES, 6]), two("f_moments", [128, TILES, 2])
        f_var, f_rstd, f_shift = (two(n, [128, TILES]) for n in ("f_var", "f_rstd", "f_shift"))

        psP = [pb(f"psP{i}", [128, 512]) for i in range(2)]
        psB = pb("psB", [128, 4, 512])
        psL = [psB[:, i, :] for i in range(2)]
        psT = psB[:, 2:4, :]
        psO = pb("psO", [128, UB, 512])
        O0, O1 = psO[:, 0, :], psO[:, 1, :]

        flat = lambda t: t.rearrange("p a b -> p (a b)")
        unflat = lambda t: t.rearrange("p (b t) -> p b t", b=UB)
        lay = lambda t: t.rearrange("p (c s) -> p c s", s=L)

        FIRST_LOOPED, END_LOOPED = 3, UNITS - 3

        class At:
            def __init__(self, off, regs=None):
                self.off, self.regs = off, regs
                self.par = (off + (FIRST_LOOPED if regs else 0)) % 2

            def to(self, d):
                return At(self.off + d, self.regs)

            def count(self, d):
                n = self.off + d
                return n if self.regs is None else self.regs[n]

            @property
            def index(self):
                return self.count(0)

        def done(eng, name, u):
            eng.wait_ge(sem(name), u.count(1))

        def before(eng, name, u, back=1):
            if u.regs is None and u.off + 1 - back < 1:
                return
            eng.wait_ge(sem(name), u.count(1 - back))

        def pipeline(eng, body):
            n = lambda u: At(u) if 0 <= u < UNITS else None
            for u in range(-2, FIRST_LOOPED):
                body(n(u + 2), n(u + 1), n(u), n(u - 1))
            with eng.Fori(FIRST_LOOPED, END_LOOPED, 2) as u:
                regs = {0: u}
                for d in range(-3, 6):
                    if d:
                        regs[d] = eng.snap(u + d)
                for p in range(2):
                    a = At(p, regs)
                    body(a.to(2), a.to(1), a, a.to(-1))
            for u in range(END_LOOPED, UNITS + 1):
                body(n(u + 2), n(u + 1), n(u), n(u - 1))

        block = ctx.enter_context(nc.Block())

        @block.sync
        def _(sp):
            sp.dma_start(mats[:, :], mats_dram).then_inc(sem("weights"), 16)
            sp.dma_start(cols[:, :], cols_dram).then_inc(sem("weights"), 16)
            sp.dma_start(masks[:, :, :], masks_dram).then_inc(sem("weights"), 16)
            sp.dma_start(w2_sb[:, :, :, :], w2_dram).then_inc(sem("expert_weights"), 16)
            def load_h(u):
                sp.wait_ge(sem("h_turned"), u + 1)
                sp.dma_start(h_tok[:, :, :], hid_v[:, bass.ds(u * TILES, TILES), :]).then_inc(sem("h_in"), 16)

            def load_res(u):
                sp.wait_ge(sem("h_res_used"), u + 1)
                sp.dma_start(h_res[:, :, :], hid_v[:, bass.ds(u * TILES, TILES), :]).then_inc(sem("h_res_in"), 16)
            load_h(0)
            load_h(1)
            with sp.Fori(0, UNITS - 2) as u:
                load_h(u + 2)
                load_res(u)
            load_res(UNITS - 2)
            load_res(UNITS - 1)
            sp.wait_ge(sem("base_out"), UNITS)
            sp.dma_start(b2_sb, b2_dram).then_inc(sem("expert_weights"), 16)
            for p in range(2):
                sp.wait_ge(sem(f"scattered{p}"), UNITS // 2 * TILES * TOPK * 16)
            sp.wait_ge(sem("pad_at"), 1)
            sp.wait_ge(sem("pad_rows"), 1)
            sp.dma_start(rows_dram[EXPERTS * CAP:EXPERTS * CAP + ST, :].rearrange("(s p) c -> p s c", p=128),
                         pad_rows[:, :, :]).then_inc(sem("padded"), 16)
            for e in range(EXPERTS):
                at = sp.value_load(pad_at[0:1, e:e + 1], min_val=e * CAP, max_val=e * CAP + N)
                sp.dma_start(rows_dram[bass.ds(at, ST), :].rearrange("(s p) c -> p s c", p=128),
                             pad_rows[:, :, :]).then_inc(sem("padded"), 16)
            sp.wait_ge(sem("padded"), (EXPERTS + 1) * 16)
            sp.wait_ge(sem("tile_table"), 1)

            def load_w1(j, i):
                for t in range(2):
                    if not (isinstance(j, int) and j < W_RING):
                        sp.wait_ge(sem("e_hid"), j + (t + 1 - W_RING))
                    sp.nop(nofuse=True)
                    e = sp.value_load(tile_ei[0:1, bass.ds(j + t, 1)], min_val=0, max_val=EXPERTS - 1)
                    sp.dma_start(w1b[(i + t) % W_RING], w1_dram[bass.ds(e, 1), :, :].rearrange("e p n -> (e p) n")).then_inc(sem(f"e_w1_in{i // 2 % 2}"), 16)

            def load_rows(j, i):
                if not (isinstance(j, int) and j < RING):
                    sp.wait_ge(sem(f"e_back{i // 2}"), (j - i) * (2 * SUB * 16 // RING))
                for t in range(2):
                    sp.nop(nofuse=True)
                    r = sp.value_load(tile_ri[0:1, bass.ds(j + t, 1)], min_val=0, max_val=EXPERTS * CAP)
                    sp.dma_start(row_in[i + t], rows_dram[bass.ds(r, ST), :].rearrange("(s p) c -> p s c", p=128)).then_inc(sem(f"e_rows_in{i // 2}"), 16)
            for j in range(0, RING, 2):
                load_rows(j, j)
                if j < W_RING:
                    load_w1(j, j)
            with sp.Fori(0, ETILES // RING - 1) as ring:
                for i in range(0, RING, 2):
                    load_w1(sp.snap(ring * RING + (i + W_RING)), (i + W_RING) % RING)
                    load_rows(sp.snap(ring * RING + (i + RING)), i)
            for j in range(ETILES - RING + W_RING, ETILES, 2):
                load_w1(j, j % RING)
            for q in range(RING // 2):
                sp.wait_ge(sem(f"e_back{q}"), ETILES // RING * 2 * SUB * 16)

            def load_back(u, i):
                sp.dma_start(back[i], back_v[:, bass.ds(u * TILES, TILES), :]).then_inc(sem(f"back_in{i}"), 16)
            for u in range(BACK_RING):
                load_back(u, u)
            with sp.Fori(1, UNITS // BACK_RING) as ring:
                for i in range(BACK_RING):
                    u = sp.snap(ring * BACK_RING + i)
                    sp.wait_ge(sem("f_sum"), u + (1 - BACK_RING))
                    sp.nop(nofuse=True)
                    load_back(u, i)

        @block.tensor
        def _(pe):
            mm = nc.tensor.matmul
            pe.wait_ge(sem("weights"), 48)

            def by_seq(ps, w, x):
                pe.nop(nofuse=True)
                for b in range(UB):
                    i = mm(ps[64 * b:64 * b + 64, 0:T], w, x[:, b, :], start=True, stop=True)
                return i

            def mix(u, n):
                if n < 4:
                    w, a = mat("x_out_a")[32 * n:32 * n + 32, :], adapt1a[32 * n:32 * n + 32, :]
                else:
                    w, a = mat("x_out_b"), adapt1b[:, :]
                kw = {"tile_position": (96, 0)} if n == 3 else {}
                mm(psP[MIX_BANK[n]][:, :], w, a, start=True, stop=True, **kw).then_inc(sem(f"mix_ps{n}"))

            def a_turn(u):
                pe.wait_ge(sem("h_in"), u.count(1) * 16)
                before(pe, "gate", u)
                for j in range(TILES):
                    last = nc.tensor.transpose(psP[0][:, j * 128:(j + 1) * 128], h_tok[:, j, :], mat("ident"))
                last.then_inc(sem("h_turned"))

            def a_adapt0(u):
                before(pe, "v_feat", u)
                done(pe, "x_lerp", u)
                mm(psP[1][0:RANK, :], mat("xl_w1"), flat(x_lerp), start=True, stop=True).then_inc(sem("adapt0_ps"))

            def a_adapt1(u):
                done(pe, "adapt0", u)
                mm(psP[0][:, :], mat("xl_w2")[:, 0:128], adapt0[:, :], start=True, stop=True)
                mm(psP[1][0:RANK, :], mat("xl_w2")[:, 128:160], adapt0[:, :], start=True, stop=True).then_inc(sem("adapt1_ps"))

            def a_mix_w_r(u):
                done(pe, "adapt1", u)
                mix(u, MIX_W)
                mix(u, MIX_R)

            def a_decay_hid(u):
                done(pe, f"mixed{MIX_W}", u)
                by_seq(psP[0], mat("w_w1"), mixed[0]).then_inc(sem("decay_hid_ps"))

            def a_mix_k(u):
                done(pe, f"mixed{MIX_R}", u)
                mix(u, MIX_K)

            def a_r(u):
                done(pe, "decay_hid", u)
                by_seq(psP[0], mat("r_w"), mixed[1]).then_inc(sem("r_ps"))

            def a_w(u):
                done(pe, f"mixed{MIX_K}", u)
                pe.nop(nofuse=True)
                for b in range(UB):
                    p = slice(GATE * b, GATE * (b + 1))
                    last = mm(psP[1][p, 0:T], mat("w_w2")[p, :], decay_hid[p, :], start=True, stop=True)
                last.then_inc(sem("w_ps"))

            def a_mix_v(u):
                done(pe, "r_done", u)
                mix(u, MIX_V)

            def a_k(u):
                done(pe, "exp_w", u)
                by_seq(psP[1], mat("k_w"), mixed[0]).then_inc(sem("k_ps"))

            def a_mix_g(u):
                done(pe, f"mixed{MIX_V}", u)
                mix(u, MIX_G)

            def a_v(u):
                done(pe, "k_done", u)
                mm(psP[1][:, :], mat("v_w"), flat(mixed[1]), start=True, stop=True).then_inc(sem("v_ps"))

            def a_g(u):
                done(pe, f"mixed{MIX_G}", u)
                mm(psP[0][:, :], mat("g_w"), flat(mixed[0]), start=True, stop=True).then_inc(sem("g_ps"))

            def b_level(u, j):
                m = lv[max(j - 1, 0)]
                R = R1[u.par] if m == "1" else Rl[m]
                done(pe, f"k_heads{j}", u)
                if j >= 2:
                    done(pe, f"r{m}", u)
                    done(pe, f"pair{j - 2}", u)
                else:
                    done(pe, "r_done", u)
                    before(pe, f"pair{4 + j}", u)
                for c in range(NC):
                    last = mm(unflat(psL[j % 2])[:, :, c * L:(c + 1) * L], k_heads[j % 2][:, c, :, :].rearrange("p h s -> p (h s)"),
                              R[:, :, c * L:(c + 1) * L], start=True, stop=True)
                last.then_inc(sem(f"level_ps{j}"))

            def b_k_tok(u):
                done(pe, "k_heads6", u)
                before(pe, "state", u)
                for c in range(NC):
                    last = nc.tensor.transpose(psT[:, c // 4, (c % 4) * 128:(c % 4 + 1) * 128],
                                               k_heads[0][:, c, :, :].rearrange("p h s -> p (h s)"), mat("ident"))
                last.then_inc(sem("k_tok_ps"))

            def b_kv(u):
                done(pe, "k_tok", u)
                done(pe, "v_tok", u)
                kv = psT[:, 0, 0:DV * NC].rearrange("p (v c) -> p v c", c=NC)
                for b in range(UB):
                    for c in range(NC):
                        last = mm(kv[64 * b:64 * b + 64, :, c], k_tok[:, c, 64 * b:64 * b + 64], v_tok[u.par][:, b * NC + c, :],
                                  start=True, stop=True)
                last.then_inc(sem("kv_ps"))

            def b_o(u, c_unit):
                done(pe, "state_heads", u)
                done(pe, "v_block", u)
                done(pe, "r32", u)
                if c_unit is not None:
                    done(pe, "base_out", c_unit)
                else:
                    before(pe, "o_sb", u)
                for c in range(NC):
                    o = unflat(O0)[:, :, c * L:(c + 1) * L]
                    if c:
                        mm(o, state_heads[:, c, :, :].rearrange("p h v -> p (h v)"), Rl["32"][:, :, c * L:(c + 1) * L],
                           start=True, stop=False)
                    for b in range(UB):
                        last = mm(o[:, b, :], v_block[:, b * NC + c, :, :].rearrange("p h v -> p (h v)"), pair[:, b, c * L:(c + 1) * L],
                                  start=(c == 0), stop=(c == 0 or b == UB - 1))
                last.then_inc(sem("o_ps"))

            def c_mean(u):
                done(pe, "o_sb", u)
                mm(O0, mat("head_mean"), o_sb[u.par][:, :], start=True, stop=True).then_inc(sem("mean_ps"))

            def c_var(u):
                done(pe, "o_sq", u)
                mm(O1, mat("head_mean"), o_sq, start=True, stop=True).then_inc(sem("var_ps"))

            def c_attn(u):
                done(pe, "o_gated", u)
                for j in range(TILES):
                    last = mm(O0[:, j * 128:(j + 1) * 128], o_gated[:, j * 128:(j + 1) * 128], mat("o_w"), start=True, stop=True)
                last.then_inc(sem("attn_ps"))

            def c_turn(u):
                done(pe, "x1", u)
                for j in range(TILES):
                    last = nc.tensor.transpose(O1[:, j * 128:(j + 1) * 128], rows[0][u.par][:, j, 0:C], mat("ident"))
                last.then_inc(sem("x1T_ps"))

            def c_logits(u):
                done(pe, "x1T", u)
                for j in range(TILES):
                    last = mm(O0[:, j * EXPERTS:(j + 1) * EXPERTS], x1T[:, j * 128:(j + 1) * 128], mat("router_w"), start=True, stop=True)
                last.then_inc(sem("logits_ps"))

            def c_place(u):
                done(pe, "seen", u)
                ps = O0[:, 64:64 + TILES * EXPERTS]
                mm(ps, mat("before"), either[:, :, :].rearrange("p n e -> p (n e)"), start=True, stop=False)
                mm(ps, mat("ones"), seen[:, 0:TILES, :].rearrange("p n e -> p (n e)"), start=False, stop=True).then_inc(sem("place_ps"))

            def c_up(u, c):
                if c == 0:
                    done(pe, "x1T", u)
                elif c == 1:
                    done(pe, "place", u)
                else:
                    done(pe, f"hid{c - 2}", u)
                mm(O1 if c % 2 == 0 else O0, mat("shared_w1")[:, c * 128:(c + 1) * 128], x1T[:, :], start=True, stop=True).then_inc(sem(f"hid_ps{c}"))

            def c_down(u):
                for c in range(HC):
                    done(pe, f"hid{c}", u)
                for j in range(TILES):
                    for c in range(HC):
                        last = mm(O0[:, j * 128:(j + 1) * 128], hid[:, c, j * 128:(j + 1) * 128],
                                  mat("shared_w2")[:, c * 128:(c + 1) * 128], start=(c == 0), stop=(c == HC - 1))
                last.then_inc(sem("down_ps"))

            def body(d, a, b, c):
                if c: c_mean(c)
                if b: b_level(b, 1)
                if a: a_adapt1(a)
                if c: c_var(c)
                if b: b_level(b, 2)
                if a: a_mix_w_r(a)
                if b: b_level(b, 3)
                if a: a_decay_hid(a)
                if a: a_mix_k(a)
                if c: c_attn(c)
                if b: b_level(b, 4)
                if a: a_r(a)
                if a: a_w(a)
                if c: c_turn(c)
                if b: b_level(b, 5)
                if c: c_logits(c)
                if c: c_up(c, 0)
                if a: a_mix_v(a)
                if c: c_place(c)
                if b: b_k_tok(b)
                if c: c_up(c, 1)
                if a: a_k(a)
                if c: c_up(c, 2)
                if a: a_mix_g(a)
                if b: b_kv(b)
                if c: c_up(c, 3)
                if a: a_v(a)
                if a: a_g(a)
                if c: c_down(c)
                if d: a_turn(d)
                if a: b_level(a, 0)
                if b: b_o(b, c)
                if d: a_adapt0(d)

            pipeline(pe, body)
            pe.wait_ge(sem("base_out"), UNITS)
            pe.nop(nofuse=True)
            mm(O0[0:32, 0:EXPERTS], mat("ones")[:, 0:32], seen[:, TILES, :], start=True, stop=True).then_inc(sem("counts_ps"))

            pe.wait_ge(sem("expert_weights"), 32)
            pe.wait_ge(sem("tile_table"), 1)
            up_ps = lambda p: psB[:, 2 * p:2 * p + 2, :]

            def e_turn(j, i):
                pe.wait_ge(sem(f"e_rows_in{i // 2}"), (j - i) * (32 // RING) + 32)
                for s in range(SUB):
                    last = nc.tensor.transpose(psP[i % 2][:, s * 128:(s + 1) * 128], row_in[i][:, s, 0:C], mat("ident"))
                last.then_inc(sem("e_turn_ps"))

            def e_up(j, i):
                p = i % 2
                pe.wait_ge(sem(f"e_w1_in{i // 2 % 2}"), (j - i % W_RING) * (32 // W_RING) + 32)
                pe.wait_ge(sem("e_xT"), j + 1)
                for c in range(HC):
                    last = mm(up_ps(p)[:, c // 2, (c % 2) * ST:(c % 2 + 1) * ST], w1b[i % W_RING][:, c * 128:(c + 1) * 128], xTe[p],
                              start=True, stop=True)
                last.then_inc(sem("e_up_ps"))

            def e_down(j, i):
                p = i % 2
                pe.wait_ge(sem("e_hid"), j + 1)
                e = pe.value_load(tile_ei[0:1, bass.ds(j, 1)], min_val=0, max_val=EXPERTS - 1)
                for s in range(SUB):
                    for c in range(HC):
                        last = mm(psO[:, p, s * 128:(s + 1) * 128], hide[p][:, c, s * 128:(s + 1) * 128],
                                  w2_sb[:, bass.ds(e, 1), c, :].rearrange("p e c -> p (e c)"), start=(c == 0), stop=(c == HC - 1))
                last.then_inc(sem("e_down_ps"))

            e_turn(0, 0)
            e_turn(1, 1)
            e_up(0, 0)
            with pe.Fori(0, ETILES // RING - 1) as ring:
                for i in range(RING):
                    e_turn(pe.snap(ring * RING + (i + 2)), (i + 2) % RING)
                    e_up(pe.snap(ring * RING + (i + 1)), (i + 1) % RING)
                    e_down(pe.snap(ring * RING + i), i)
            for j in range(ETILES - RING, ETILES):
                if j + 2 < ETILES:
                    e_turn(j + 2, (j + 2) % RING)
                if j + 1 < ETILES:
                    e_up(j + 1, (j + 1) % RING)
                e_down(j, j % RING)

        @block.scalar
        def _(act):
            A = nc.scalar.activation
            act.wait_ge(sem("weights"), 48)
            act.wait_ge(sem("head_bonus"), 1)
            act.wait_ge(sem("zeroed"), 1)

            def a_adapt0(u):
                done(act, "adapt0_ps", u)
                A(adapt0[:, :], psP[1][0:RANK, :], ACT.Tanh).then_inc(sem("adapt0"))

            def a_adapt1(u):
                done(act, "adapt1_ps", u)
                A(adapt1a[:, :], psP[0][:, :], ACT.Tanh, bias=col("xl_b2a"))
                A(adapt1b[:, :], psP[1][0:RANK, :], ACT.Tanh, bias=col("xl_b2b", RANK)).then_inc(sem("adapt1"))

            def a_decay_hid(u):
                done(act, "decay_hid_ps", u)
                A(decay_hid[:, :], psP[0][:, 0:T], ACT.Tanh).then_inc(sem("decay_hid"))

            def a_r(u):
                done(act, "r_ps", u)
                before(act, "level_ps1", u, 2)
                for b in range(UB):
                    last = A(R1[u.par][64 * b:64 * b + 64, b, :], psP[0][64 * b:64 * b + 64, 0:T], ACT.Copy)
                last.then_inc(sem("r_done"))

            def a_w(u):
                done(act, "w_ps", u)
                before(act, "decay", u)
                A(exp_w[:, :], psP[1][:, 0:T], ACT.Exp, bias=col("w_b")).then_inc(sem("exp_w"))

            def a_decay(u):
                done(act, "exp_w", u)
                before(act, "tot2", u, 2)
                A(tot1[u.par][:, :], exp_w[:, :], ACT.Exp, scale=-1.0).then_inc(sem("decay"))

            def a_k(u):
                done(act, "k_ps", u)
                before(act, "r2", u, 2)
                A(K1[u.par][:, :], psP[1][:, 0:T], ACT.Copy).then_inc(sem("k_done"))

            def a_v(u):
                done(act, "v_ps", u)
                before(act, "v_tok", u)
                A(v_feat[:, :], psP[1][:, :], ACT.Copy).then_inc(sem("v_feat"))

            def a_g(u):
                done(act, "g_ps", u)
                before(act, "o_gated", u, 2)
                A(gate[u.par][:, :], psP[0][:, :], ACT.Tanh, scale=0.5).then_inc(sem("gate_tanh"))

            def b_v_block(u):
                done(act, "v_tok", u)
                before(act, "o_ps", u)
                for h in range(NH):
                    p = slice(32 * h, 32 * h + 32)
                    last = A(v_block[p, :, h, :], v_tok[u.par][p, :, :], ACT.Copy)
                last.then_inc(sem("v_block"))

            def b_k_heads(u, j):
                m = lv[max(j - 1, 0)]
                K = K1[u.par] if m == "1" else Kl[m]
                if j >= 2:
                    done(act, f"level_ps{j - 2}", u)
                else:
                    before(act, "k_tok_ps" if j == 0 else "level_ps5", u)
                if j == 0:
                    done(act, "k_done", u)
                if j > 1:
                    done(act, f"r{m}", u)
                for h in range(NH):
                    last = A(k_heads[j % 2][:, :, h, :], lay(K[:, :]), ACT.Copy,
                             scale=head_bonus[:, h:h + 1] if j == 0 else col(f"head{h}"))
                last.then_inc(sem(f"k_heads{j}"))

            def b_k_tok(u):
                done(act, "k_tok_ps", u)
                A(k_tok[:, :, :], psT[:, :, :].rearrange("p b (c k) -> p (b c) k", k=128), ACT.Copy).then_inc(sem("k_tok"))

            def b_state_heads(u):
                done(act, "state", u)
                before(act, "o_ps", u)
                for h in range(NH):
                    last = A(state_heads[:, 1:NC, h, :], state[:, :, 0:NC - 1].rearrange("p v c -> p c v"), ACT.Copy, scale=col(f"head{h}"))
                last.then_inc(sem("state_heads"))

            def b_o(u):
                done(act, "o_ps", u)
                A(o_sb[u.par][:, :], O0, ACT.Copy).then_inc(sem("o_sb"))

            def c_sq(u):
                done(act, "o_cent", u)
                A(o_sq, o_cent, ACT.Square).then_inc(sem("o_sq"))

            def c_std(u):
                done(act, "var_ps", u)
                A(o_std, O1, ACT.Ln, bias=eps[:, 0:1]).then_inc(sem("o_log"))
                done(act, "o_log", u)
                A(o_std, o_std, ACT.Exp, scale=-0.5).then_inc(sem("o_std"))

            def c_aff(u):
                done(act, "o_norm", u)
                A(o_aff[:, :], o_norm, ACT.Identity, bias=col("gn_b"), scale=col("gn_w")).then_inc(sem("o_aff"))

            def c_x1T(u):
                done(act, "x1T_ps", u)
                A(x1T[:, :], O1, ACT.Copy).then_inc(sem("x1T"))

            def c_top_exp(u):
                done(act, "top_gap", u)
                A(top_exp[:, :], top_gap[:, :], ACT.Exp).then_inc(sem("top_exp"))

            def c_hid(u, c):
                done(act, f"hid_ps{c}", u)
                A(hid[:, c, :], O1 if c % 2 == 0 else O0, ACT.Relu, bias=col(f"shared_b1_{c}")).then_inc(sem(f"hid{c}"))

            def body(d, a, b, c):
                if a: a_adapt0(a)
                if b: b_k_heads(b, 2)
                if c: c_sq(c)
                if b: b_v_block(b)
                if a: a_adapt1(a)
                if b: b_k_heads(b, 3)
                if c: c_std(c)
                if c: c_aff(c)
                if a: a_decay_hid(a)
                if b: b_k_heads(b, 4)
                if a: a_r(a)
                if b: b_k_heads(b, 5)
                if a: a_w(a)
                if a: a_decay(a)
                if c: c_x1T(c)
                if c: c_top_exp(c)
                if c: c_hid(c, 0)
                if b: b_k_heads(b, 6)
                if c: c_hid(c, 1)
                if a: a_k(a)
                if b: b_k_tok(b)
                if c: c_hid(c, 2)
                if c: c_hid(c, 3)
                if a: a_v(a)
                if a: a_g(a)
                if b: b_state_heads(b)
                if a: b_k_heads(a, 0)
                if a: b_k_heads(a, 1)
                if b: b_o(b)

            pipeline(act, body)

            def e_hid(j, i):
                p = i % 2
                act.wait_ge(sem("e_up_ps"), j + 1)
                for c in range(HC):
                    last = A(hide[p][:, c, :], psB[:, 2 * p + c // 2, (c % 2) * ST:(c % 2 + 1) * ST], ACT.Relu,
                             bias=w1b[i % W_RING][:, HIDDEN + c:HIDDEN + c + 1])
                last.then_inc(sem("e_hid"))

            def e_weigh(j, i):
                p = i % 2
                act.wait_ge(sem("e_y"), j + 1)
                for s in range(SUB):
                    last = A(yw[i][:, s, :], ye[p][:, s, :], ACT.Copy, scale=row_in[i][:, s, AT_W:AT_W + 1])
                last.then_inc(sem("e_yw"))

            e_hid(0, 0)
            with act.Fori(0, ETILES // RING - 1) as ring:
                for i in range(RING):
                    e_hid(act.snap(ring * RING + (i + 1)), (i + 1) % RING)
                    e_weigh(act.snap(ring * RING + i), i)
            for j in range(ETILES - RING, ETILES):
                if j + 1 < ETILES:
                    e_hid(j + 1, (j + 1) % RING)
                e_weigh(j, j % RING)

            with act.Fori(0, UNITS // 2) as half_u:
                for p in range(2):
                    u = act.snap(half_u * 2 + p)
                    act.wait_ge(sem("f_shift"), u + 1)
                    act.wait_ge(sem(f"stored{p}"), half_u * 16 + 16)
                    for j in range(TILES):
                        last = A(f_out[p][:, j, :], f_z[p][:, j * C:(j + 1) * C], ACT.Identity,
                                 bias=f_shift[p][:, j:j + 1], scale=f_rstd[p][:, j:j + 1])
                    last.then_inc(sem("f_out"))
                    act.wait_ge(sem("f_out"), u + 3)
                    act.dma_start(out_v[:, bass.ds(u * TILES, TILES), :], f_out[p]).then_inc(sem(f"stored{p}"), 16)
            for p in range(2):
                act.wait_ge(sem(f"stored{p}"), UNITS // 2 * 16 + 16)

        @block.gpsimd
        def _(pool):
            G = nc.gpsimd
            pool.sem_inc(sem("h_turned"), 1)
            pool.sem_inc(sem("stored0"), 16)
            pool.sem_inc(sem("stored1"), 16)
            pool.sem_inc(sem("h_res_used"), 1)
            pool.sem_inc(sem("f_out"), 2)
            for m in lv[:-1]:
                G.memset(r_fac[m][:, :, 0], 1.0)
                G.memset(k_fac[m][:, :, 1], 1.0)
            G.memset(chunk_decay[:, :, 0], 0.0)
            G.memset(eps[:, :], EPS)
            G.memset(minus_half[:, :], -0.5)
            G.memset(hT[:, :, 0:1], 0.0)
            G.memset(seen[:, 0, :], 0.0)
            G.memset(ones_row[:, :], 1.0)
            for k in range(TOPK):
                for p in range(2):
                    G.memset(rows[k][p][:, :, :], 0.0)
            G.memset(pad_rows[:, :, :], 0.0)
            for R in [*R1, *Rl.values()]:
                G.memset(R[:, :, :], 0.0)
            G.memset(v_block[:, :, :, :], 0.0).then_inc(sem("zeroed"))
            pool.wait_ge(sem("weights"), 48)
            pool.wait_ge(sem("zeroed"), 1)
            G.tensor_copy(dest[:, :, :].rearrange("p n k -> p (n k)"), mat("token_no")).then_inc(sem("dest0"))
            G.iota(pad_rows[:, :, AT_DEST:AT_DEST + 1].bitcast(i32), pattern=[[0, SUB], [1, 1]], base=TRASH, channel_multiplier=1).then_inc(sem("pad_rows"))

            def b_factor(u, i):
                m, m2 = lv[i], lv[i + 1]
                w = int(m)
                t_m, K, R = (tot1[u.par], K1[u.par], R1[u.par]) if w == 1 else (tot[m], Kl[m], Rl[m])
                pairs = t_m[:, :].rearrange("p (n two) -> p n two", two=2)
                blocks = lambda t: t.rearrange("p (n w) -> p n w", w=w)
                fac = lambda t: t.rearrange("p n two -> p (n two)").unsqueeze(2).broadcast_to([128, T // w, w])
                if w > 1:
                    done(pool, f"tot{m}", u)
                else:
                    done(pool, "decay", u)
                    before(pool, "chunk_decay", u)
                pool.nop(nofuse=True)
                G.tensor_copy(r_fac[m][:, :, 1], pairs[:, :, 0])
                G.tensor_copy(k_fac[m][:, :, 0], pairs[:, :, 1])
                G.tensor_tensor(tot[m2][:, :], pairs[:, :, 0], pairs[:, :, 1], ALU.mult).then_inc(sem(f"tot{m2}"))
                if w == 1:
                    done(pool, "k_done", u)
                    done(pool, "r_done", u)
                else:
                    done(pool, f"r{m}", u)
                done(pool, f"tot{m2}", u)
                before(pool, f"k_heads{i + 2}", u)
                G.tensor_tensor(blocks(Kl[m2][:, :]), blocks(K[:, :]), fac(k_fac[m][:, :, :]), ALU.mult)
                before(pool, f"level_ps{i + 2}" if m2 != "32" else "o_ps", u)
                both = lambda t: t.rearrange("p b (n w) -> p b n w", w=w)
                G.tensor_tensor(both(Rl[m2][:, :, :]), both(R[:, :, :]),
                                fac(r_fac[m][:, :, :]).unsqueeze(1).broadcast_to([128, UB, T // w, w]), ALU.mult).then_inc(sem(f"r{m2}"))

            def b_chunk_decay(u):
                done(pool, "tot32", u)
                before(pool, "state", u)
                pool.nop(nofuse=True)
                G.tensor_copy(chunk_decay[:, :, 1:NC],
                              tot["32"][:, 1:NC].unsqueeze(1).broadcast_to([128, DV, NC - 1])).then_inc(sem("chunk_decay"))

            def c_rstd(u):
                done(pool, "moments", u)
                pool.nop(nofuse=True)
                G.tensor_scalar(z_var[:, :], moments[:, :, 1], EPS, None, ALU.add).then_inc(sem("var_eps"))
                done(pool, "var_eps", u)
                G.tensor_tensor(z_rstd[:, :], z_var[:, :], minus_half[:, :], ALU.pow).then_inc(sem("z_rstd"))

            def c_rows(u):
                done(pool, "x1", u)
                pool.nop(nofuse=True)
                G.tensor_copy(rows[1][u.par][:, :, 0:C], rows[0][u.par][:, :, 0:C]).then_inc(sem("rows1"))
                G.tensor_tensor(base_out[:, bass.ds(u.index * TILES, TILES), :], rows[0][u.par][:, :, 0:C], mat("shared_b2").unsqueeze(1).broadcast_to([128, TILES, C]),
                                ALU.add).then_inc(sem("x1_b2"))

            def c_scatter(u):
                done(pool, "slots", u)
                done(pool, "rows1", u)
                pool.nop(nofuse=True)
                for j in range(TILES):
                    for k in range(TOPK):
                        G.indirect_dma_start(rows_dram[:, :], bass.IndirectOffsetOnAxis(slot[u.par][:, j, k:k + 1], 0),
                                             rows[k][u.par][:, j, :], None).then_inc(sem(f"scattered{u.par}"), 16)

            def body(d, a, b, c):
                if b: b_factor(b, 0)
                if b: b_factor(b, 1)
                if b: b_factor(b, 2)
                if b: b_factor(b, 3)
                if b: b_factor(b, 4)
                if b: b_chunk_decay(b)
                if c: c_rstd(c)
                if c: c_rows(c)
                if c: c_scatter(c)

            pipeline(pool, body)

            with pool.Fori(0, ETILES // RING) as ring:
                for i in range(RING):
                    pool.wait_ge(sem("e_yw"), ring * RING + (i + 1))
                    pool.nop(nofuse=True)
                    for s in range(SUB):
                        G.indirect_dma_start(back_dram[:, :], bass.IndirectOffsetOnAxis(row_in[i][:, s, AT_DEST:AT_DEST + 1].bitcast(u32), 0),
                                             yw[i][:, s, :], None, bounds_check=TRASH - 1, oob_is_err=False).then_inc(sem(f"e_back{i // 2}"), 16)

            with pool.Fori(0, UNITS // 2) as half_u:
                for p in range(2):
                    u = pool.snap(half_u * 2 + p)
                    pool.wait_ge(sem("f_moments"), u + 1)
                    pool.nop(nofuse=True)
                    G.tensor_scalar(f_shift[p][:, :], f_moments[p][:, :, 0], -1.0, None, ALU.mult)
                    G.tensor_scalar(f_var[p][:, :], f_moments[p][:, :, 1], EPS, None, ALU.add).then_inc(sem("f_var_eps"))
                    pool.wait_ge(sem("f_var_eps"), u + 1)
                    G.tensor_tensor(f_rstd[p][:, :], f_var[p][:, :], minus_half[:, :], ALU.pow).then_inc(sem("f_rstd"))
                    pool.wait_ge(sem("f_rstd"), u + 1)
                    G.tensor_tensor(f_shift[p][:, :], f_shift[p][:, :], f_rstd[p][:, :], ALU.mult).then_inc(sem("f_shift"))

        @block.vector
        def _(dve):
            V = nc.vector
            dve.wait_ge(sem("weights"), 48)
            V.tensor_scalar(head_bonus[:, :], cols[:, COL["head0"]:COL["head0"] + NH], col("bonus"), None, ALU.mult).then_inc(sem("head_bonus"))
            dve.wait_ge(sem("zeroed"), 1)
            dve.wait_ge(sem("dest0"), 1)

            def a_delta(u):
                dve.wait_ge(sem("h_turned"), u.count(2))
                before(dve, f"mixed{MIX_G}", u)
                V.tensor_copy(hT[:, :, 1:T + 1], unflat(psP[0][:, :])).then_inc(sem("hT"))
                done(dve, "hT", u)
                V.tensor_tensor(delta[:, :, :], hT[:, :, 0:T], hT[:, :, 1:T + 1], ALU.subtract).then_inc(sem("delta"))
                done(dve, "delta", u)
                before(dve, "adapt0_ps", u)
                V.scalar_tensor_tensor(x_lerp[:, :, :], delta[:, :, :], col("x_mu"), hT[:, :, 1:T + 1], ALU.mult, ALU.add).then_inc(sem("x_lerp"))

            def a_mixed(u, i):
                n = MIX_ORDER[i]
                done(dve, f"mix_ps{n}", u)
                if i >= 2:
                    done(dve, ["decay_hid_ps", "r_ps", "k_ps"][i - 2], u)
                else:
                    before(dve, ["g_ps", "v_ps"][i], u)
                V.scalar_tensor_tensor(mixed[i % 2][:, :, :], unflat(psP[MIX_BANK[n]][:, :]),
                                       col(f"x_bias{n}"), delta[:, :, :], ALU.add, ALU.mult).then_inc(sem("mixed_delta"))
                dve.wait_ge(sem("mixed_delta"), u.index * NMIX + (i + 1))
                V.tensor_tensor(mixed[i % 2][:, :, :], mixed[i % 2][:, :, :], hT[:, :, 1:T + 1], ALU.add).then_inc(sem(f"mixed{n}"))

            def a_v_tok(u):
                done(dve, "v_feat", u)
                before(dve, "kv_ps", u, 2)
                V.transpose(v_tok[u.par][:, :, :].rearrange("p n v -> p (n v)"), v_feat[:, :]).then_inc(sem("v_tok"))

            def a_gate(u):
                done(dve, "gate_tanh", u)
                V.scalar_tensor_tensor(gate[u.par][:, :], gate[u.par][:, :], 1.0, psP[0][:, :], ALU.add, ALU.mult).then_inc(sem("gate"))

            def b_pair(u, j):
                done(dve, f"level_ps{j}", u)
                ps = psL[j % 2].rearrange("p (c t) -> p c t", t=L)
                to = pair[:, :, :].rearrange("p b (c t) -> p (b c) t", t=L)
                if j == 0:
                    before(dve, "o_ps", u)
                    m = mat("diag").unsqueeze(1).broadcast_to([128, UB * NC, L])
                    V.tensor_tensor(to, ps, m, ALU.mult).then_inc(sem("pair0"))
                else:
                    m = masks[:, j - 1, :].unsqueeze(1).broadcast_to([128, UB * NC, L])
                    done(dve, f"pair{j - 1}", u)
                    dve.nop(nofuse=True)
                    V.copy_predicated(to, m, ps).then_inc(sem(f"pair{j}"))

            def b_state(u):
                done(dve, "kv_ps", u)
                done(dve, "chunk_decay", u)
                before(dve, "state_heads", u)
                V.tensor_tensor_scan(state[:, :, :].rearrange("p v c -> p (v c)"), chunk_decay[:, :, :].rearrange("p v c -> p (v c)"),
                                     psT[:, 0, 0:DV * NC], 0.0, ALU.mult, ALU.add).then_inc(sem("state"))

            def c_cent(u):
                done(dve, "mean_ps", u)
                before(dve, "o_aff", u)
                V.tensor_tensor(o_cent, o_sb[u.par][:, :], O0, ALU.subtract).then_inc(sem("o_cent"))

            def c_norm(u):
                done(dve, "o_std", u)
                V.tensor_tensor(o_norm, o_cent, o_std, ALU.mult).then_inc(sem("o_norm"))

            def c_gated(u):
                done(dve, "o_aff", u)
                before(dve, "attn_ps", u)
                V.scalar_tensor_tensor(o_gated[:, :], o_aff[:, :], 0.5, gate[u.par][:, :], ALU.mult, ALU.mult).then_inc(sem("o_gated"))

            def c_z(u):
                done(dve, "attn_ps", u)
                dve.wait_ge(sem("h_res_in"), u.count(1) * 16)
                before(dve, "x1", u)
                V.tensor_tensor(flat(z[:, :, :]), O0, flat(h_res[:, :, :]), ALU.add).then_inc(sem("h_res_used"))
                dve.wait_ge(sem("h_res_used"), u.count(2))
                for j in range(TILES):
                    last = V.bn_stats(stats[:, j, :], z[:, j, :])
                last.then_inc(sem("stats"))
                done(dve, "stats", u)
                dve.nop(nofuse=True)
                for j in range(TILES):
                    last = V.bn_aggr(moments[:, j, :], stats[:, j, :])
                last.then_inc(sem("moments"))

            def scattered(u, back):
                if u.regs is None and u.off + 1 - back < 1:
                    return
                dve.wait_ge(sem(f"scattered{u.par}"), u.count(-u.par) * (TILES * TOPK * 8))

            def c_x1(u):
                done(dve, "z_rstd", u)
                scattered(u, 2)
                before(dve, "rows1", u, 2)
                for j in range(TILES):
                    last = V.tensor_scalar(rows[0][u.par][:, j, 0:C], z[:, j, :], moments[:, j, 0:1], z_rstd[:, j:j + 1],
                                           ALU.subtract, ALU.mult)
                last.then_inc(sem("x1"))

            ROUTE = ["logits", "top_val", "top_idf", "chosen", "either", "seen0", "seen1", "seen2",
                     "place_of", "slot_f", "top_sum", "top_w0", "dest_out"]

            def routed(u, name):
                dve.wait_ge(sem("route_steps"), u.index * len(ROUTE) + (ROUTE.index(name) + 1))

            def c_top(u):
                done(dve, "logits_ps", u)
                before(dve, "slots", u)
                V.tensor_tensor(logits[:, :, :], O0[:, 0:TILES * EXPERTS].rearrange("p (n e) -> p n e", e=EXPERTS),
                                mat("expert_bias").unsqueeze(1).broadcast_to([128, TILES, EXPERTS]), ALU.add).then_inc(sem("route_steps"))
                routed(u, "logits")
                dve.nop(nofuse=True)
                for j in range(TILES):
                    last = V.max(top_val[:, j, :], logits[:, j, :])
                last.then_inc(sem("route_steps"))
                routed(u, "top_val")
                dve.nop(nofuse=True)
                for j in range(TILES):
                    last = V.max_index(top_idx[:, j, :], top_val[:, j, :], logits[:, j, :])
                V.tensor_tensor(top_gap[:, :], top_val[:, :, 1], top_val[:, :, 0], ALU.subtract).then_inc(sem("top_gap"))
                done(dve, "top_gap", u)
                V.tensor_copy(top_idf[:, :, :], top_idx[:, :, 0:TOPK]).then_inc(sem("route_steps"))
                routed(u, "top_idf")
                V.tensor_tensor(chosen[:, :, :, :], top_idf[:, :, :].unsqueeze(3).broadcast_to([128, TILES, TOPK, EXPERTS]),
                                mat("expert_no").unsqueeze(1).unsqueeze(1).broadcast_to([128, TILES, TOPK, EXPERTS]),
                                ALU.is_equal).then_inc(sem("route_steps"))
                routed(u, "chosen")
                V.tensor_tensor(either[:, :, :], chosen[:, :, 0, :], chosen[:, :, 1, :], ALU.add).then_inc(sem("route_steps"))
                routed(u, "either")
                for j in range(TILES):
                    V.tensor_tensor(seen[:, j + 1, :], seen[:, j, :], either[:, j, :], ALU.add).then_inc(sem("route_steps" if j < TILES - 1 else "seen"))
                    if j < TILES - 1:
                        routed(u, f"seen{j}")

            def c_slots(u):
                done(dve, "place_ps", u)
                V.tensor_tensor(place[:, :, :], O0[:, 64:64 + TILES * EXPERTS].rearrange("p (n e) -> p n e", e=EXPERTS),
                                mat("region").unsqueeze(1).broadcast_to([128, TILES, EXPERTS]), ALU.add).then_inc(sem("place"))
                V.tensor_copy(seen[:, 0, :], seen[:, TILES, :])
                done(dve, "place", u)
                V.tensor_tensor(place_of[:, :, :, :], chosen[:, :, :, :], place[:, :, :].unsqueeze(2).broadcast_to([128, TILES, TOPK, EXPERTS]),
                                ALU.mult).then_inc(sem("route_steps"))
                routed(u, "place_of")
                V.tensor_reduce(slot_f[:, :, :], place_of[:, :, :, :], AX.X, ALU.add).then_inc(sem("route_steps"))
                routed(u, "slot_f")
                scattered(u, 2)
                V.tensor_copy(slot[u.par][:, :, :], slot_f[:, :, :])
                done(dve, "top_exp", u)
                V.tensor_scalar(top_sum[:, :], top_exp[:, :], 1.0, None, ALU.add).then_inc(sem("route_steps"))
                routed(u, "top_sum")
                V.reciprocal(top_w0[:, :], top_sum[:, :]).then_inc(sem("route_steps"))
                routed(u, "top_w0")
                V.tensor_copy(rows[0][u.par][:, :, AT_W], top_w0[:, :])
                V.tensor_tensor(rows[1][u.par][:, :, AT_W], top_w0[:, :], top_exp[:, :], ALU.mult)
                for k in range(TOPK):
                    last = V.tensor_copy(rows[k][u.par][:, :, AT_DEST].bitcast(i32), dest[:, :, k])
                last.then_inc(sem("route_steps"))
                routed(u, "dest_out")
                V.tensor_scalar(dest[:, :, :], dest[:, :, :], float(TOPK * UT), None, ALU.add).then_inc(sem("slots"))

            def c_base(u):
                done(dve, "down_ps", u)
                done(dve, "x1_b2", u)
                b = base_out[:, bass.ds(u.index * TILES, TILES), :].rearrange("p n c -> p (n c)")
                V.tensor_tensor(b, O0, b, ALU.add).then_inc(sem("base_out"))

            def body(d, a, b, c):
                if c: c_cent(c)
                if b: b_pair(b, 0)
                if b: b_pair(b, 1)
                if b: b_pair(b, 2)
                if a: a_mixed(a, 0)
                if a: a_mixed(a, 1)
                if c: c_norm(c)
                if c: c_gated(c)
                if b: b_pair(b, 3)
                if a: a_mixed(a, 2)
                if c: c_z(c)
                if c: c_x1(c)
                if b: b_pair(b, 4)
                if b: b_pair(b, 5)
                if c: c_top(c)
                if a: a_mixed(a, 3)
                if c: c_slots(c)
                if a: a_mixed(a, 4)
                if b: b_state(b)
                if a: a_v_tok(a)
                if a: a_gate(a)
                if c: c_base(c)
                if d: a_delta(d)

            pipeline(dve, body)

            step = [0]

            def link(ins):
                step[0] += 1
                ins.then_inc(sem("table_step"))
                dve.wait_ge(sem("table_step"), step[0])

            dve.wait_ge(sem("counts_ps"), 1)
            link(V.tensor_copy(counts[:, :], O0[0:1, 0:EXPERTS]))
            link(V.tensor_scalar(tiles_f[:, :], counts[:, :], float(ST - 1), None, ALU.add))
            link(V.tensor_copy(ci[:, 0, :], tiles_f[:, :]))
            link(V.tensor_scalar(ci[:, 1, :], ci[:, 0, :], ST.bit_length() - 1, None, ALU.logical_shift_right))
            link(V.tensor_copy(tiles_f[:, :], ci[:, 1, :]))
            link(V.tensor_tensor_scan(tiles_to[:, :], ones_row[:, :], tiles_f[:, :], 0.0, ALU.mult, ALU.add))
            link(V.tensor_tensor(pad_at_f[:, :], counts[:, :], mat("region")[0:1, :], ALU.add))
            V.tensor_copy(pad_at[:, :], pad_at_f[:, :]).then_inc(sem("pad_at"))
            t_bc = mat("tile_no").unsqueeze(2).broadcast_to([1, ETILES, EXPERTS])
            link(V.tensor_tensor(past, t_bc, tiles_to[:, :].unsqueeze(1).broadcast_to([1, ETILES, EXPERTS]), ALU.is_ge))
            link(V.tensor_reduce(tile_e[:, :], past, AX.X, ALU.add))
            link(V.tensor_tensor(past, past, tiles_f[:, :].unsqueeze(1).broadcast_to([1, ETILES, EXPERTS]), ALU.mult))
            link(V.tensor_reduce(tile_s[:, :], past, AX.X, ALU.add))
            link(V.tensor_tensor(tile_s[:, :], mat("tile_no"), tile_s[:, :], ALU.subtract))
            link(V.tensor_scalar(tile_v[:, :], tile_e[:, :], float(EXPERTS), float(ST), ALU.is_lt, ALU.mult))
            link(V.tensor_tensor(tile_s[:, :], tile_s[:, :], tile_v[:, :], ALU.mult))
            link(V.tensor_scalar(tile_v[:, :], tile_e[:, :], float(CAP), None, ALU.mult))
            link(V.tensor_tensor(tile_s[:, :], tile_s[:, :], tile_v[:, :], ALU.add))
            link(V.tensor_scalar(tile_e[:, :], tile_e[:, :], float(EXPERTS - 1), None, ALU.min))
            link(V.tensor_copy(tile_ri[:, :], tile_s[:, :]))
            V.tensor_copy(tile_ei[:, :], tile_e[:, :]).then_inc(sem("tile_table"))
            dve.wait_ge(sem("tile_table"), 1)
            dve.wait_ge(sem("expert_weights"), 32)

            def e_xT(j, p):
                dve.wait_ge(sem("e_turn_ps"), j + 1)
                V.tensor_copy(xTe[p], psP[p][:, 0:ST]).then_inc(sem("e_xT"))

            def e_y(j, p):
                dve.wait_ge(sem("e_down_ps"), j + 1)
                e = dve.value_load(tile_ei[0:1, bass.ds(j, 1)], min_val=0, max_val=EXPERTS - 1)
                V.tensor_tensor(ye[p], psO[:, p, 0:ST].rearrange("p (s c) -> p s c", c=C),
                                b2_sb[:, bass.ds(e, 1), :].broadcast_to([128, SUB, C]), ALU.add).then_inc(sem("e_y"))

            e_xT(0, 0)
            e_xT(1, 1)
            with dve.Fori(0, ETILES // 2 - 1) as half_j:
                for p in range(2):
                    dve.wait_ge(sem("e_up_ps"), half_j * 2 + (p + 1))
                    e_xT(dve.snap(half_j * 2 + (p + 2)), p)
                    e_y(dve.snap(half_j * 2 + p), p)
            for j in range(ETILES - 2, ETILES):
                e_y(j, j % 2)

            with dve.Fori(0, UNITS // BACK_RING) as ring:
                for i in range(BACK_RING):
                    p = i % 2
                    u = dve.snap(ring * BACK_RING + i)
                    dve.wait_ge(sem(f"back_in{i}"), ring * 16 + 16)
                    V.tensor_tensor(f_sum[p].rearrange("p (n c) -> p n c", c=C), back[i][:, :, 0:C], back[i][:, :, C:2 * C],
                                    ALU.add).then_inc(sem("f_sum"))
                    dve.wait_ge(sem("f_sum"), u + 1)
                    dve.wait_ge(sem("f_out"), u + 1)
                    V.tensor_tensor(f_z[p], f_sum[p], base_out[:, bass.ds(u * TILES, TILES), :].rearrange("p n c -> p (n c)"),
                                    ALU.add).then_inc(sem("f_z"))
                    dve.wait_ge(sem("f_z"), u + 1)
                    for j in range(TILES):
                        last = V.bn_stats(f_stats[p][:, j, :], f_z[p][:, j * C:(j + 1) * C])
                    last.then_inc(sem("f_stats"))
                    dve.wait_ge(sem("f_stats"), u + 1)
                    dve.nop(nofuse=True)
                    for j in range(TILES):
                        last = V.bn_aggr(f_moments[p][:, j, :], f_stats[p][:, j, :])
                    last.then_inc(sem("f_moments"))


def pack(i):
    m = np.zeros((128, MAT_COLS), np.float32)

    def put(name, a):
        r, c = MATS[name]
        m[:r, MAT_AT[name]:MAT_AT[name] + c] = a
    g = lambda n: np.asarray(i["L0_attn_" + n])
    f = lambda n: np.asarray(i["L0_ffn_" + n])
    put("xl_w1", g("xl_w1").T)
    put("xl_w2", g("xl_w2").T)
    put("x_out_a", g("x_out_w").T[:128])
    put("x_out_b", g("x_out_w").T[128:])
    for n in ("r_w", "k_w", "w_w1", "v_w", "g_w", "o_w"):
        put(n, g(n).T)
    put("w_w2", np.tile(g("w_w2").T, (UB, 1)))
    p = np.arange(128)
    put("ident", np.eye(128, dtype=np.float32))
    put("head_mean", (p[:, None] // DV == p[None, :] // DV).astype(np.float32) / DV)
    put("diag", (p[:, None] % L == np.arange(L)[None, :]).astype(np.float32))
    put("before", (p[:, None] < p[None, :]).astype(np.float32))
    put("ones", np.ones((128, 128), np.float32))
    put("router_w", f("router_w"))
    put("expert_bias", np.broadcast_to(f("expert_bias"), (128, EXPERTS)))
    put("expert_no", np.broadcast_to(np.arange(EXPERTS, dtype=np.float32), (128, EXPERTS)))
    put("region", np.broadcast_to(np.arange(EXPERTS, dtype=np.float32) * CAP, (128, EXPERTS)))
    n = (np.arange(TILES)[None, :, None] * 128 + p[:, None, None]) * TOPK + np.arange(TOPK)
    put("token_no", n.reshape(128, -1).astype(np.float32))
    put("tile_no", np.arange(ETILES, dtype=np.float32)[None])
    put("shared_b2", np.broadcast_to(f("shared_b2")[0], (128, C)))
    put("shared_w1", f("shared_w1")[0])
    put("shared_w2", f("shared_w2")[0].reshape(HC, 128, C).transpose(1, 0, 2).reshape(128, HIDDEN))
    c = np.zeros((128, len(COLS)), np.float32)

    def putc(name, a):
        c[:len(a), COL[name]] = a
    putc("x_mu", g("x_proj_mu"))
    putc("xl_b2a", g("xl_b2")[:128])
    putc("xl_b2b", g("xl_b2")[128:])
    for n in range(NMIX):
        putc(f"x_bias{n}", g("x_bias")[n])
    putc("w_b", np.tile(g("w_b"), UB))
    putc("bonus", np.tile(g("bonus").reshape(-1), UB))
    putc("gn_w", g("gn_weight"))
    putc("gn_b", g("gn_bias"))
    for h in range(NH):
        putc(f"head{h}", ((p % HK) // DK == h).astype(np.float32))
    for h in range(HC):
        putc(f"shared_b1_{h}", f("shared_b1")[0][h * 128:(h + 1) * 128])
    s, t = p[:, None] % L, np.arange(L)[None, :]
    masks = np.stack([((s // w) % 2 == 0) & (t // w == s // w + 1) for w in HALVES], 1).astype(np.uint32)
    b1 = f("routed_b1").reshape(EXPERTS, HC, 128).transpose(0, 2, 1)
    w1 = np.ascontiguousarray(np.concatenate([f("routed_w1"), b1], axis=2))
    w2 = np.ascontiguousarray(f("routed_w2").reshape(EXPERTS, HC, 128, C).transpose(2, 0, 1, 3))
    b2 = np.ascontiguousarray(np.broadcast_to(f("routed_b2"), (128, EXPERTS, C)))
    return {"in_mats": m, "in_cols": c, "in_masks": masks, "in_w1": w1, "in_w2": w2, "in_b2": b2}


def kernel(**inputs):
    import concourse.bacc as _bacc
    from concourse.bass_utils import run_bass_kernel_spmd as _run
    nc = _bacc.Bacc("TRN2", target_bir_lowering=False, num_devices=1)
    arrays = {"in_hidden": np.ascontiguousarray(inputs["L0_attn_hidden_states"]), **pack(inputs)}
    aps = [nc.dram_tensor(n, a.shape, mybir.dt.from_np(a.dtype), kind="ExternalInput").ap() for n, a in arrays.items()]
    out = nc.dram_tensor("out", (SEQS, T, C), mybir.dt.float32, kind="ExternalOutput").ap()
    build(nc, *aps, out)
    r = _run(nc, [arrays], core_ids=[0])
    return r.results[0]["out"]
```
